# Optimizing a Trainium2 kernel written in Bass

```python
import numpy as np
import jax
import jax.numpy as jnp

def _softmax(x, axis=-1):
    return jax.nn.softmax(x, axis=axis)

def _gelu(x):
    return jax.nn.gelu(x, approximate=True)

def _silu(x):
    return jax.nn.silu(x)

def _sigmoid(x):
    return jax.nn.sigmoid(x)

def _layernorm(x, axis=-1, eps=1e-05):
    m = jnp.mean(x, axis=axis, keepdims=True)
    v = jnp.var(x, axis=axis, keepdims=True)
    return (x - m) / jnp.sqrt(v + eps)

def _scatter_add(tgt, idx, src, axis=0):
    return tgt.at[idx].add(src)

def _segment_sum(src, seg, n):
    return jax.ops.segment_sum(src, seg, n)
kernel_name = 'mk_adaln_d1_jaxref_r4_da528c'

def setup_inputs(seed: int=0):
    np.random.seed(seed)
    _w = jnp.asarray

    def _L0_attn_setup():
        import jax, jax.numpy as jnp
        import numpy as np
        from jax import lax
        D_MODEL = 256
        KERNEL = 5
        PAD = (KERNEL - 1) // 2
        key = jax.random.key(seed)
        k1, k2, k3, k4, k5 = jax.random.split(key, 5)
        B, T, D = (8, 1024, D_MODEL)
        x = jax.random.normal(k1, (B, T, D), dtype=jnp.float32)
        decay_logit = jnp.zeros((D,), dtype=jnp.float32)
        lim = 1.0 / np.sqrt(D)
        W = jax.random.uniform(k2, (D, D), minval=-lim, maxval=lim, dtype=jnp.float32)
        b = jax.random.uniform(k3, (D,), minval=-lim, maxval=lim, dtype=jnp.float32)
        limc = 1.0 / np.sqrt(KERNEL)
        conv_w = jax.random.uniform(k4, (D, 1, KERNEL), minval=-limc, maxval=limc, dtype=jnp.float32)
        conv_b = jax.random.uniform(k5, (D,), minval=-limc, maxval=limc, dtype=jnp.float32)
        return {'x': x, 'decay_logit': decay_logit, 'W': W, 'b': b, 'conv_w': conv_w, 'conv_b': conv_b}
    _L0_attn_in = _L0_attn_setup()

    def _L0_ffn_setup():
        import jax, jax.numpy as jnp
        import numpy as np
        B, S, H = (8, 1024, 256)
        NAV = 128
        E = 8
        F = 2 * H
        key = jax.random.key(seed)
        ks = jax.random.split(key, 12)

        def w(k, shape, fan_in):
            return jax.random.normal(k, shape, dtype=jnp.float32) / np.sqrt(fan_in)
        return {'hidden_states': jax.random.normal(ks[0], (B, S, H), dtype=jnp.float32), 'Wp1': w(ks[1], (H, NAV), H), 'bp1': jnp.zeros((NAV,), jnp.float32), 'Wp2': w(ks[2], (NAV, E), NAV), 'bp2': jnp.zeros((E,), jnp.float32), 'W1': w(ks[3], (E, H, F), H), 'b1': jnp.zeros((E, F), jnp.float32), 'W2': w(ks[4], (E, F, H), F), 'b2': jnp.zeros((E, H), jnp.float32), 'Wo': w(ks[5], (H, H), H), 'bo': jnp.zeros((H,), jnp.float32)}
    _L0_ffn_in = _L0_ffn_setup()
    _L0_c = _w((lambda *s: np.random.randn(*s).astype(np.float32) * 0.05)(32, 256))
    _L0_wmod = _w((lambda *s: np.random.randn(*s).astype(np.float32) * 0.05)(256, 6 * 256) * 256 ** (-0.5))
    _d = {'L0_attn_x': _L0_attn_in['x'], 'L0_attn_decay_logit': _L0_attn_in['decay_logit'], 'L0_attn_W': _L0_attn_in['W'], 'L0_attn_b': _L0_attn_in['b'], 'L0_attn_conv_w': _L0_attn_in['conv_w'], 'L0_attn_conv_b': _L0_attn_in['conv_b'], 'L0_ffn_Wp1': _L0_ffn_in['Wp1'], 'L0_ffn_bp1': _L0_ffn_in['bp1'], 'L0_ffn_Wp2': _L0_ffn_in['Wp2'], 'L0_ffn_bp2': _L0_ffn_in['bp2'], 'L0_ffn_W1': _L0_ffn_in['W1'], 'L0_ffn_b1': _L0_ffn_in['b1'], 'L0_ffn_W2': _L0_ffn_in['W2'], 'L0_ffn_b2': _L0_ffn_in['b2'], 'L0_ffn_Wo': _L0_ffn_in['Wo'], 'L0_ffn_bo': _L0_ffn_in['bo'], 'L0_c': _L0_c, 'L0_wmod': _L0_wmod}
    _x0 = _d['L0_attn_x']
    _d['L0_attn_x'] = jax.random.normal(jax.random.fold_in(jax.random.key(seed), 1), (32, 512, 256), dtype=_x0.dtype)
    del _x0
    return _d

def reference(L0_attn_x, L0_attn_decay_logit, L0_attn_W, L0_attn_b, L0_attn_conv_w, L0_attn_conv_b, L0_ffn_Wp1, L0_ffn_bp1, L0_ffn_Wp2, L0_ffn_bp2, L0_ffn_W1, L0_ffn_b1, L0_ffn_W2, L0_ffn_b2, L0_ffn_Wo, L0_ffn_bo, L0_c, L0_wmod):

    def _L0_attn_ref(x, decay_logit, W, b, conv_w, conv_b):
        import jax, jax.numpy as jnp
        import numpy as np
        from jax import lax
        D_MODEL = 256
        KERNEL = 5
        PAD = (KERNEL - 1) // 2
        B, T, D = x.shape
        a = jax.nn.sigmoid(decay_logit)

        def step(s, xt):
            s = a * s + (1.0 - a) * xt
            return (s, s)
        s0 = jnp.zeros((B, D), dtype=x.dtype)
        _, S = lax.scan(step, s0, jnp.swapaxes(x, 0, 1))
        y_ret = jnp.einsum('tbd,ed->tbe', S, W) + b
        y_ret = jnp.swapaxes(y_ret, 0, 1)
        xc = jnp.swapaxes(x, 1, 2)
        y_loc = lax.conv_general_dilated(xc, conv_w, window_strides=(1,), padding=[(PAD, PAD)], feature_group_count=D)
        y_loc = y_loc + conv_b[None, :, None]
        y_loc = jnp.swapaxes(y_loc, 1, 2)
        return y_ret + y_loc

    def _L0_ffn_ref(hidden_states, Wp1, bp1, Wp2, bp2, W1, b1, W2, b2, Wo, bo):
        import jax, jax.numpy as jnp
        import numpy as np
        B, S, H = (8, 1024, 256)
        NAV = 128
        E = 8
        F = 2 * H
        last = hidden_states[:, -1, :]
        logits = jax.nn.gelu(last @ Wp1 + bp1, approximate=False) @ Wp2 + bp2
        action_probs = jax.nn.softmax(logits, axis=-1)
        sel = jnp.argmax(action_probs, axis=-1)
        w1 = W1[sel]
        w2 = W2[sel]
        h = jax.nn.gelu(jnp.einsum('bsh,bhf->bsf', hidden_states, w1) + b1[sel][:, None, :], approximate=False)
        reasoned = jnp.einsum('bsf,bfh->bsh', h, w2) + b2[sel][:, None, :]
        out = reasoned @ Wo + bo
        return hidden_states + 0.3 * out
    x = L0_attn_x
    mod = (_silu(L0_c) @ L0_wmod).reshape(L0_c.shape[0], 6, 1, -1)
    sa, ca, ga, sb, cb, gb = (mod[:, 0], mod[:, 1], mod[:, 2], mod[:, 3], mod[:, 4], mod[:, 5])
    ga = (2 * (ga >= 0) - 1) * jnp.maximum(jnp.abs(ga), 0.25)
    gb = (2 * (gb >= 0) - 1) * jnp.maximum(jnp.abs(gb), 0.25)
    h = _layernorm(x, axis=-1) * (1 + ca) + sa
    x = x + ga * _L0_attn_ref(h, L0_attn_decay_logit, L0_attn_W, L0_attn_b, L0_attn_conv_w, L0_attn_conv_b)
    h = _layernorm(x, axis=-1) * (1 + cb) + sb
    x = x + gb * _L0_ffn_ref(h, L0_ffn_Wp1, L0_ffn_bp1, L0_ffn_Wp2, L0_ffn_bp2, L0_ffn_W1, L0_ffn_b1, L0_ffn_W2, L0_ffn_b2, L0_ffn_Wo, L0_ffn_bo)
    return x

_drawn_inputs = setup_inputs


def setup_inputs(seed=0):
    import zlib

    import numpy as np

    out = dict(_drawn_inputs(seed))
    spreads = {'L0_attn_decay_logit': (0.0, 2.0),
     'L0_ffn_bp1': (0.0, 0.48),
     'L0_ffn_bp2': (0.0, 0.1),
     'L0_ffn_b1': (0.0, 0.8),
     'L0_ffn_b2': (0.0, 0.8),
     'L0_ffn_bo': (0.0, 0.8)}
    factors = {'L0_attn_b': 4.527}
    for name, (base, spread) in spreads.items():
        noise = np.random.default_rng([zlib.crc32(name.encode()), seed]).standard_normal(out[name].shape)
        drawn = base * np.exp(spread * noise) if base else spread * noise
        out[name] = jnp.asarray(drawn.astype(out[name].dtype))
    for name, factor in factors.items():
        out[name] = (out[name] * factor).astype(out[name].dtype)
    return out
```

```python
import concourse.bass as bass
from concourse import mybir
from contextlib import ExitStack


def adaln_attention_ffn_kernel(nc, x, decay_logit, W, b, conv_w, conv_b, Wp1, bp1, Wp2, bp2,
                               W1, b1, W2, b2, Wo, bo, c_in, wmod, out):
    f32 = mybir.dt.float32
    f32r = mybir.dt.float32r
    u32 = mybir.dt.uint32
    ALU = mybir.AluOpType
    ACT = mybir.ActivationFunctionType

    P = 128
    B, T, D = x.shape
    E, _, F = W1.shape
    NAV = Wp1.shape[1]
    TAPS = conv_w.shape[2]
    PAD = (TAPS - 1) // 2
    TT = T // P
    DC = D // P
    FC = F // P
    TPB = 512 // D
    HB = TT // TPB
    EPS = 1e-5
    OUT_SCALE = 0.3
    GATE_MIN = 0.25
    CA, SA, GA, GAB, CB, SB = (DC * n for n in range(6))
    MODS = 6 * DC
    PACK = FC * D + FC

    down_table = nc.dram_tensor("down_table", (E, P, PACK), f32, kind="Internal").ap()
    beta_table = nc.dram_tensor("beta_table", (E, 2, D), f32, kind="Internal").ap()
    gate_table = nc.dram_tensor("gate_table", (B, D), f32, kind="Internal").ap()

    def tok(dram):
        return dram.rearrange("(t p) d -> p t d", p=P)

    with ExitStack() as ctx:
        def sb(name, shape, dt=f32):
            return ctx.enter_context(nc.sbuf_tensor(name, shape, dt))

        def bank(name):
            return ctx.enter_context(nc.psum_tensor(name, [P, 512], f32))

        def sem(name):
            return ctx.enter_context(nc.semaphore(name))

        ident = sb("ident", [P, P])
        ones_r = sb("ones_r", [P, P], f32r)
        decay = sb("decay", [P, DC])
        keep = sb("keep", [P, DC])
        fresh = sb("fresh", [P, DC])
        w_nat = sb("w_nat", [P, DC, D])
        mixT = sb("mixT", [P, DC, D])
        taps = sb("taps", [P, DC, TAPS])
        bias_b = sb("bias_b", [P, DC])
        bias_c = sb("bias_c", [P, DC])
        bias_bc = sb("bias_bc", [P, DC])
        wp1 = sb("wp1", [P, DC, NAV])
        bp1_sb = sb("bp1_sb", [P, 1])
        wp2 = sb("wp2", [P, E])
        bp2_sb = sb("bp2_sb", [1, E])
        wo = sb("wo", [P, DC, D])
        b1_all = sb("b1_all", [P, E, FC])
        b2_all = sb("b2_all", [P, DC, E])
        bo_all = sb("bo_all", [E, D])
        c_nat = sb("c_nat", [B, D])
        silu_cT = sb("silu_cT", [P, DC, B])
        wmod_sb = sb("wmod_sb", [P, DC, 6 * D])
        mods = sb("mods", [P, B, MODS])
        gate_raw = sb("gate_raw", [P, DC, B])
        gate_sign = sb("gate_sign", [P, DC, B])
        gate_size = sb("gate_size", [P, DC, B])
        gate = sb("gate", [P, DC, B])
        gb_raw = sb("gb_raw", [B, D])
        gb_sign = sb("gb_sign", [B, D])
        gb_size = sb("gb_size", [B, D])
        gb_rows = sb("gb_rows", [B, D])
        beta = sb("beta", [E, D])
        beta3 = sb("beta3", [E, D])
        beta_parts = sb("beta_parts", [E, 2, D], f32r)
        w2_nat = sb("w2_nat", [P, 2, FC, D])
        w2T = sb("w2T", [P, 2, DC, F])
        pack = sb("pack", [P, 2, PACK])
        eps_t = sb("eps_t", [P, TT])
        minus_half = sb("minus_half", [P, TT])
        minus_one = sb("minus_one", [P, TT])

        x_sb = sb("x_sb", [P, 2, TT, D])
        modc = sb("modc", [P, 2, MODS])
        st1 = sb("st1", [P, TT, 6])
        mv1 = sb("mv1", [P, TT, 2])
        ve1 = sb("ve1", [P, TT])
        rstd1 = sb("rstd1", [P, TT])
        mr1 = sb("mr1", [P, TT])
        nmr1 = sb("nmr1", [P, TT])
        xn1 = sb("xn1", [P, TT, D])
        h = sb("h", [P, DC, T + 2 * PAD])
        S = sb("S", [P, DC, T])
        r1T = sb("r1T", [P, DC, T])
        x1 = sb("x1", [P, 2, TT, D])
        st2 = sb("st2", [P, TT, 6])
        mv2 = sb("mv2", [P, TT, 2])
        ve2 = sb("ve2", [P, TT])
        rstd2 = sb("rstd2", [P, TT])
        mr2 = sb("mr2", [P, TT])
        nmr2 = sb("nmr2", [P, TT])
        xn2 = sb("xn2", [P, TT, D])
        hid = sb("hid", [P, 2, DC, T])
        nav = sb("nav", [P, 1])
        logits = sb("logits", [1, E])
        top8 = sb("top8", [1, 8])
        sel8 = sb("sel8", [1, 2, 8], u32)
        up_w = sb("up_w", [P, 2, DC, F])
        down_w = sb("down_w", [P, 2, PACK])
        beta_w = sb("beta_w", [P, 2, D], f32r)
        hg = sb("hg", [P, FC, T])
        gb_bc = sb("gb_bc", [P, 2, D])
        o_sb = sb("o_sb", [P, 2, TT, D])

        Y = [bank("Y0"), bank("Y1")]
        TR = [bank("TR0"), bank("TR1")]
        U = [bank("U0"), bank("U1")]
        Q = [bank("Q0"), bank("Q1")]

        s_setup = sem("s_setup")
        s_wmod = sem("s_wmod")
        s_w2 = [sem("s_w2a"), sem("s_w2b")]
        s_pool_const = sem("s_pool_const")
        s_pe_setup = sem("s_pe_setup")
        s_act_setup = sem("s_act_setup")
        s_dve_setup = sem("s_dve_setup")
        s_tables = sem("s_tables")
        s_w2T_mm = sem("s_w2T_mm")
        s_w2T_cp = sem("s_w2T_cp")
        s_comb = sem("s_comb")
        s_pack = sem("s_pack")
        s_packed_out = [sem("s_packed_a"), sem("s_packed_b")]

        x_loaded = [sem("x_loaded0"), sem("x_loaded1")]
        gb_loaded = [sem("gb_loaded0"), sem("gb_loaded1")]
        w_loaded = [sem("w_loaded0"), sem("w_loaded1")]
        stored = [sem("stored0"), sem("stored1")]
        modc_ready = sem("modc_ready")
        dve_st1 = sem("dve_st1")
        stats1_ready = sem("stats1_ready")
        pool_rstd1 = sem("pool_rstd1")
        norm1_ready = sem("norm1_ready")
        xn1_ready = sem("xn1_ready")
        t1_done = sem("t1_done")
        h_ready = sem("h_ready")
        S_ready = sem("S_ready")
        mix_done = sem("mix_done")
        conv_step = sem("conv_step")
        conv_done = sem("conv_done")
        r1_ready = sem("r1_ready")
        t2_done = sem("t2_done")
        x1_ready = sem("x1_ready")
        dve_st2 = sem("dve_st2")
        stats2_ready = sem("stats2_ready")
        pool_rstd2 = sem("pool_rstd2")
        norm2_ready = sem("norm2_ready")
        xn2_ready = sem("xn2_ready")
        t3_done = sem("t3_done")
        hid_ready = sem("hid_ready")
        r_nav = sem("r_nav")
        nav_ready = sem("nav_ready")
        r_logits = sem("r_logits")
        dve_router = sem("dve_router")
        sel_ready = sem("sel_ready")
        up_done = sem("up_done")
        gelu_ready = sem("gelu_ready")
        down_done = sem("down_done")
        scaled = sem("scaled")
        o_ready = sem("o_ready")

        SETUP_LOADED = 16 * (12 + E + DC)
        GATES_DONE = 16
        SETUP_STEPS = GATES_DONE + 2 * DC + 4

        def wait(eng, s, v):
            if not isinstance(v, int) or v > 0:
                eng.wait_ge(s, v)

        def snapped(eng, v):
            return v if isinstance(v, int) else eng.snap(eng.to_reg(v), min_val=0, max_val=4096)

        def slots(eng, slot):
            for i in range(-2, 4):
                slot(i, i // 2, i % 2)
            with eng.Fori(2, B // 2 - 2) as m:
                slot(2 * m, m, 0)
                slot(2 * m + 1, m, 1)
            for i in range(B - 4, B + 1):
                slot(i, i // 2, i % 2)

        def inside(i, off):
            return not isinstance(i, int) or 0 <= i + off < B

        block = ctx.enter_context(nc.Block())

        @block.sync
        def _(sp):
            def load_x(i, half, par):
                wait(sp, x1_ready, 2 * (i - 1))
                sp.dma_start(x_sb[:, par], tok(x[bass.ds(i, 1)].rearrange("o t d -> (o t) d"))).then_inc(x_loaded[par], 16)

            load_x(0, 0, 0)
            load_x(1, 0, 1)
            small = [(decay[:, :], decay_logit.rearrange("(c p) -> p c", p=P)),
                     (w_nat[:, :, :], W.rearrange("(c p) d -> p c d", p=P)),
                     (c_nat[:, :], c_in),
                     (taps[:, :, :], conv_w.rearrange("(c p) o k -> p c (o k)", p=P)),
                     (bias_b[:, :], b.rearrange("(c p) -> p c", p=P)),
                     (bias_c[:, :], conv_b.rearrange("(c p) -> p c", p=P)),
                     (wp1[:, :, :], Wp1.rearrange("(c p) n -> p c n", p=P)),
                     (bp1_sb[:, :], bp1.rearrange("(p o) -> p o", o=1)),
                     (wp2[:, :], Wp2),
                     (bp2_sb[:, :], bp2.rearrange("(o e) -> o e", o=1)),
                     (wo[:, :, :], Wo.rearrange("(c p) d -> p c d", p=P)),
                     (bo_all[:, :], bo.rearrange("(o d) -> o d", o=1).to_broadcast([E, D]))]
            with nc.allow_non_contiguous_dma(reason="small vectors onto partitions"):
                for dst, src in small:
                    sp.dma_start(dst, src).then_inc(s_setup, 16)
                for e in range(E):
                    sp.dma_start(b1_all[:, e, :], b1[e].rearrange("(c p) -> p c", p=P)).then_inc(s_setup, 16)
                for c in range(DC):
                    sp.dma_start(b2_all[:, c, :], b2[:, c * P:(c + 1) * P].rearrange("e p -> p e")).then_inc(s_setup, 16)
            sp.dma_start(wmod_sb[:, :, :], wmod.rearrange("(c p) n -> p c n", p=P)).then_inc(s_wmod, 16)

            for e in range(E):
                wait(sp, s_w2T_mm, e - 1)
                sp.dma_start(w2_nat[:, e % 2], W2[e].rearrange("(c p) d -> p c d", p=P)).then_inc(s_w2[e % 2], 16)
                if e >= 1:
                    wait(sp, s_pack, e * 2)
                    sp.dma_start(down_table[e - 1], pack[:, (e - 1) % 2]).then_inc(s_packed_out[(e - 1) % 2], 16)
            wait(sp, s_pack, E * 2)
            sp.dma_start(down_table[E - 1], pack[:, (E - 1) % 2]).then_inc(s_packed_out[(E - 1) % 2], 16)
            sp.wait_ge(s_dve_setup, SETUP_STEPS)
            sp.dma_start(gate_table, gb_rows[:, :]).then_inc(s_tables, 16)
            sp.dma_start(beta_table, beta_parts[:, :, :].bitcast(f32)).then_inc(s_tables, 16)
            sp.wait_ge(s_tables, 32)
            for q in s_packed_out:
                sp.wait_ge(q, 16 * E // 2)

            def slot(i, half, par):
                if inside(i, 0):
                    used, chosen = snapped(sp, HB * (i - 1)), snapped(sp, i + 1)
                    sp.wait_ge(s_setup, SETUP_LOADED)
                    wait(sp, down_done, used)
                    sp.wait_ge(sel_ready, chosen)
                    e = sp.value_load(sel8[0:1, par, 0:1], min_val=0, max_val=E - 1)
                    sp.dma_start(up_w[:, par], W1[bass.ds(e, 1)].rearrange("o (c p) f -> p (o c) f", p=P)).then_inc(w_loaded[par], 16)
                    sp.dma_start(down_w[:, par], down_table[bass.ds(e, 1)].rearrange("o p n -> p (o n)")).then_inc(w_loaded[par], 16)
                    sp.dma_start(beta_w[0:2, par].bitcast(f32), beta_table[bass.ds(e, 1)].rearrange("o k d -> (o k) d")).then_inc(w_loaded[par], 16)
                if inside(i, 1):
                    wait(sp, scaled, HB * i)
                    sp.dma_start(gb_bc[:, 1 - par], gate_table[bass.ds(i + 1, 1)].to_broadcast([P, D])).then_inc(gb_loaded[1 - par], 16)
                if inside(i, -1):
                    for k in range(HB):
                        sp.wait_ge(o_ready, HB * (i - 1) + k + 1)
                        ts = slice(k * TPB, (k + 1) * TPB)
                        sp.dma_start(tok(out[bass.ds(i - 1, 1)].rearrange("o t d -> (o t) d"))[:, ts], o_sb[:, 1 - par, ts]).then_inc(stored[1 - par], 16)
                if inside(i, 3) and inside(i, 1):
                    load_x(i + 3, half + 1, 1 - par)

            slots(sp, slot)
            for q in stored:
                sp.wait_ge(q, 16 * HB * B // 2)

        @block.gpsimd
        def _(pool):
            nc.gpsimd.memset(ident[:, :], 0.0).then_inc(s_pool_const, 1)
            nc.gpsimd.memset(eps_t[:, :], EPS).then_inc(s_pool_const, 1)
            nc.gpsimd.memset(minus_half[:, :], -0.5).then_inc(s_pool_const, 1)
            nc.gpsimd.memset(minus_one[:, :], -1.0).then_inc(s_pool_const, 1)
            nc.gpsimd.memset(ones_r[:, :].bitcast(f32), 1.0).then_inc(s_pool_const, 1)
            nc.gpsimd.memset(beta_w[:, :, :].bitcast(f32), 0.0).then_inc(s_pool_const, 1)
            nc.gpsimd.memset(h[:, :, :], 0.0).then_inc(s_pool_const, 1)
            pool.wait_ge(s_pool_const, 7)
            nc.gpsimd.affine_select(out=ident[:, :], in_=ident[:, :], compare_op=ALU.not_equal, fill=1.0,
                                    base=0, pattern=[[-1, P]], channel_multiplier=1).then_inc(s_pool_const, 1)

            def norm_scale(b_, stats_ready, consumed, mv, ve, rstd, mr, nmr, steps, ready):
                pool.wait_ge(stats_ready, b_ + 1)
                wait(pool, consumed, TT * b_)
                nc.gpsimd.tensor_tensor(ve[:, :], mv[:, :, 1], eps_t[:, :], ALU.add).then_inc(steps, 1)
                pool.wait_ge(steps, 3 * b_ + 1)
                nc.gpsimd.tensor_tensor(rstd[:, :], ve[:, :], minus_half[:, :], ALU.pow).then_inc(steps, 1)
                pool.wait_ge(steps, 3 * b_ + 2)
                nc.gpsimd.tensor_tensor(mr[:, :], mv[:, :, 0], rstd[:, :], ALU.mult).then_inc(steps, 1)
                pool.wait_ge(steps, 3 * b_ + 3)
                nc.gpsimd.tensor_tensor(nmr[:, :], mr[:, :], minus_one[:, :], ALU.mult).then_inc(ready, 1)

            def slot(i, half, par):
                if inside(i, 2):
                    norm_scale(i + 2, stats1_ready, xn1_ready, mv1, ve1, rstd1, mr1, nmr1, pool_rstd1, norm1_ready)
                if inside(i, 1):
                    norm_scale(i + 1, stats2_ready, xn2_ready, mv2, ve2, rstd2, mr2, nmr2, pool_rstd2, norm2_ready)

            slots(pool, slot)

        @block.scalar
        def _(act):
            act.wait_ge(s_setup, SETUP_LOADED)
            nc.scalar.activation(keep[:, :], decay[:, :], ACT.Sigmoid).then_inc(s_act_setup, 1)
            act.wait_ge(s_pe_setup, 1)
            for c in range(DC):
                nc.scalar.activation(silu_cT[:, c], Y[0][:, c * B:(c + 1) * B], ACT.Silu).then_inc(s_act_setup, 1)
            act.wait_ge(s_dve_setup, 1)
            act.wait_ge(s_pe_setup, 2)
            for c in range(DC):
                nc.scalar.activation(mixT[:, c], Y[1][:, c * D:(c + 1) * D], ACT.Copy,
                                     scale=fresh[:, c:c + 1]).then_inc(s_act_setup, 1)
            for e in range(E):
                for k in range(2):
                    act.wait_ge(s_comb, 2 * e + k + 1)
                    if e >= 2 and k == 0:
                        act.wait_ge(s_packed_out[e % 2], 16 * (e // 2))
                    n = FC // 2 * D
                    ins = nc.scalar.activation(pack[:, e % 2, k * n:(k + 1) * n], Q[k][:, :], ACT.Copy, scale=OUT_SCALE)
                    if k == 0:
                        ins.then_inc(s_pack, 1)
                    else:
                        nc.scalar.copy(pack[:, e % 2, FC * D:], b1_all[:, e, :]).then_inc(s_pack, 1)

            def normalise(b_, src, dst, rstd, nmr, scale_ready, used, ready):
                act.wait_ge(scale_ready, b_ + 1)
                wait(act, used, DC * b_)
                for j in range(TT):
                    nc.scalar.activation(dst[:, j], src[:, j], ACT.Identity, bias=nmr[:, j:j + 1],
                                         scale=rstd[:, j:j + 1]).then_inc(ready, 1)

            def slot(i, half, par):
                opp = 1 - par
                if inside(i, 0):
                    act.wait_ge(r_nav, i + 1)
                    nc.scalar.activation(nav[:, :], TR[0][:, 0:1], ACT.Gelu, bias=bp1_sb[:, 0:1]).then_inc(nav_ready, 1)
                if inside(i, 1):
                    wait(act, t2_done, HB * (i + 1))
                    for c in range(DC):
                        act.wait_ge(conv_done, DC * (i + 1) + c + 1)
                        nc.scalar.activation(r1T[:, c], Y[c][:, :], ACT.Identity, bias=modc[:, opp, GAB + c:GAB + c + 1],
                                             scale=modc[:, opp, GA + c:GA + c + 1]).then_inc(r1_ready, 1)
                if inside(i, 2):
                    normalise(i + 2, x_sb[:, par], xn1, rstd1, nmr1, norm1_ready, t1_done, xn1_ready)
                    wait(act, conv_done, DC * (i + 2))
                    act.wait_ge(modc_ready, i + 3)
                    for c in range(DC):
                        act.wait_ge(t1_done, DC * (i + 2) + c + 1)
                        nc.scalar.activation(h[:, c, PAD:PAD + T], Y[c][:, :], ACT.Identity, bias=modc[:, par, SA + c:SA + c + 1],
                                             scale=modc[:, par, CA + c:CA + c + 1]).then_inc(h_ready, 1)
                def gelus(f0, f1):
                    for f in range(f0, f1):
                        act.wait_ge(up_done, FC * i + f + 1)
                        nc.scalar.activation(hg[:, f], U[f % 2][:, :], ACT.Gelu,
                                             bias=down_w[:, par, FC * D + f:FC * D + f + 1]).then_inc(gelu_ready, 1)

                if inside(i, 0):
                    wait(act, down_done, HB * i)
                    gelus(0, FC // 2)
                if inside(i, 1):
                    normalise(i + 1, x1[:, opp], xn2, rstd2, nmr2, norm2_ready, t3_done, xn2_ready)
                if inside(i, 0):
                    gelus(FC // 2, FC)
                if inside(i, 1):
                    for c in range(DC):
                        act.wait_ge(t3_done, DC * (i + 1) + c + 1)
                        nc.scalar.activation(hid[:, opp, c], TR[c][:, :], ACT.Identity, bias=modc[:, opp, SB + c:SB + c + 1],
                                             scale=modc[:, opp, CB + c:CB + c + 1]).then_inc(hid_ready, 1)

            slots(act, slot)

        @block.vector
        def _(dve):
            step = [0]

            def done(ins):
                ins.then_inc(s_dve_setup, 1)
                step[0] += 1
                return step[0]

            dve.wait_ge(s_act_setup, 1)
            done(nc.vector.tensor_scalar(fresh[:, :], keep[:, :], -1.0, 1.0, ALU.mult, ALU.add))
            dve.wait_ge(s_setup, SETUP_LOADED)
            n = done(nc.vector.tensor_tensor(bias_bc[:, :], bias_b[:, :], bias_c[:, :], ALU.add))

            dve.wait_ge(s_pe_setup, 3)
            view = TR[0][:, 0:5 * DC * B].rearrange("p (g c r) -> p g c r", g=5, c=DC)
            m4 = mods[:, :, :].rearrange("p r (g c) -> p g c r", c=DC)
            done(nc.vector.tensor_copy(m4[:, SA // DC], view[:, 0]))
            done(nc.vector.tensor_scalar_add(m4[:, CA // DC], view[:, 1], 1.0))
            done(nc.vector.tensor_copy(m4[:, SB // DC], view[:, 3]))
            done(nc.vector.tensor_scalar_add(m4[:, CB // DC], view[:, 4], 1.0))
            n = done(nc.vector.tensor_copy(gate_raw[:, :, :], view[:, 2]))
            dve.wait_ge(s_dve_setup, n)
            done(nc.vector.tensor_scalar(gate_sign[:, :, :], gate_raw[:, :, :], 0.0, 2.0, ALU.is_ge, ALU.mult))
            n = done(nc.vector.scalar_tensor_tensor(out=gate_size[:, :, :], in0=gate_raw[:, :, :], scalar=-1.0, in1=gate_raw[:, :, :], op0=ALU.mult, op1=ALU.max))
            dve.wait_ge(s_dve_setup, n)
            n = done(nc.vector.tensor_scalar_max(gate_size[:, :, :], gate_size[:, :, :], GATE_MIN))
            dve.wait_ge(s_dve_setup, n)
            n = done(nc.vector.scalar_tensor_tensor(out=gate[:, :, :], in0=gate_sign[:, :, :], scalar=-1.0,
                                                    in1=gate_size[:, :, :], op0=ALU.add, op1=ALU.mult))
            dve.wait_ge(s_pe_setup, 4)
            n = done(nc.vector.tensor_copy(gb_raw[:, :], TR[1][0:B, 0:D]))
            dve.wait_ge(s_dve_setup, n)
            done(nc.vector.tensor_scalar(gb_sign[:, :], gb_raw[:, :], 0.0, 2.0, ALU.is_ge, ALU.mult))
            n = done(nc.vector.scalar_tensor_tensor(out=gb_size[:, :], in0=gb_raw[:, :], scalar=-1.0, in1=gb_raw[:, :], op0=ALU.mult, op1=ALU.max))
            dve.wait_ge(s_dve_setup, n)
            n = done(nc.vector.tensor_scalar_max(gb_size[:, :], gb_size[:, :], GATE_MIN))
            dve.wait_ge(s_dve_setup, n)
            n = done(nc.vector.scalar_tensor_tensor(out=gb_rows[:, :], in0=gb_sign[:, :], scalar=-1.0,
                                                    in1=gb_size[:, :], op0=ALU.add, op1=ALU.mult))
            assert n == GATES_DONE
            for c in range(DC):
                done(nc.vector.tensor_copy(mods[:, :, GA + c], gate[:, c, :]))
                n = done(nc.vector.tensor_scalar(mods[:, :, GAB + c], gate[:, c, :], bias_bc[:, c:c + 1], None, ALU.mult))
            dve.wait_ge(s_pe_setup, 5)
            n = done(nc.vector.tensor_tensor(beta[:, :], U[0][0:E, 0:D], bo_all[:, :], ALU.add))
            dve.wait_ge(s_dve_setup, n)
            n = done(nc.vector.tensor_scalar_mul(beta3[:, :], beta[:, :], OUT_SCALE))
            dve.wait_ge(s_dve_setup, n)
            n = done(nc.vector.tensor_copy(beta_parts[:, 0, :], beta3[:, :]))
            dve.wait_ge(s_dve_setup, n)
            n = done(nc.vector.tensor_tensor(beta_parts[:, 1, :], beta3[:, :], beta_parts[:, 0, :].bitcast(f32), ALU.subtract))
            dve.wait_ge(s_dve_setup, n)
            assert n == SETUP_STEPS
            for e in range(E):
                dve.wait_ge(s_w2T_mm, e + 1)
                wait(dve, s_comb, 2 * (e - 1))
                for c in range(DC):
                    nc.vector.tensor_copy(w2T[:, e % 2, c], Y[c][:, :]).then_inc(s_w2T_cp, 1)

            def conv(b_):
                for k in range(TAPS):
                    for c in range(DC):
                        if k == 0:
                            dve.wait_ge(mix_done, DC * b_ + c + 1)
                        else:
                            dve.wait_ge(conv_step, (TAPS - 1) * DC * b_ + DC * (k - 1) + c + 1)
                        ins = nc.vector.scalar_tensor_tensor(out=Y[c][:, :], in0=h[:, c, k:k + T], scalar=taps[:, c, k:k + 1],
                                                             in1=Y[c][:, :], op0=ALU.mult, op1=ALU.add)
                        ins.then_inc(conv_step if k < TAPS - 1 else conv_done, 1)

            def router(b_, par):
                dve.wait_ge(r_logits, b_ + 1)
                nc.vector.tensor_tensor(logits[:, :], TR[0][0:1, 8:8 + E], bp2_sb[:, :], ALU.add).then_inc(dve_router, 1)
                count = snapped(dve, 2 * b_ + 1)
                dve.wait_ge(s_pool_const, 8)
                dve.wait_ge(dve_router, count)
                nc.vector.max(top8[:, :], logits[:, :]).then_inc(dve_router, 1)
                count = snapped(dve, 2 * b_ + 2)
                dve.wait_ge(s_pool_const, 8)
                dve.wait_ge(dve_router, count)
                nc.vector.max_index(sel8[:, par], top8[:, :], logits[:, :]).then_inc(sel_ready, 1)

            def residual2(b_, half, par):
                for k in range(HB):
                    ts = slice(k * TPB, (k + 1) * TPB)
                    if k == 0:
                        dve.wait_ge(gb_loaded[par], 16 * (half + 1))
                        wait(dve, stored[par], 16 * HB * half)
                    dve.wait_ge(down_done, HB * b_ + k + 1)
                    nc.vector.tensor_tensor(o_sb[:, par, ts], Q[k][:, :].rearrange("p (t d) -> p t d", d=D),
                                            gb_bc[:, par:par + 1].to_broadcast([P, TPB, D]), ALU.mult).then_inc(scaled, 1)
                    dve.wait_ge(scaled, HB * b_ + k + 1)
                    nc.vector.tensor_tensor(o_sb[:, par, ts], o_sb[:, par, ts], x1[:, par, ts], ALU.add).then_inc(o_ready, 1)

            def stats1(b_, half, par):
                wait(dve, hid_ready, DC * (b_ - 1))
                nc.vector.tensor_copy(modc[:, par:par + 1, :], mods[:, bass.ds(b_, 1), :]).then_inc(modc_ready, 1)
                dve.wait_ge(x_loaded[par], 16 * (half + 1))
                for j in range(TT):
                    nc.vector.bn_stats(st1[:, j], x_sb[:, par, j]).then_inc(dve_st1, 1)
                used, full = snapped(dve, b_), snapped(dve, TT * (b_ + 1))
                dve.wait_ge(s_pool_const, 8)
                wait(dve, norm1_ready, used)
                dve.wait_ge(dve_st1, full)
                for j in range(TT):
                    ins = nc.vector.bn_aggr(mv1[:, j], st1[:, j])
                ins.then_inc(stats1_ready, 1)

            def residual1(b_, par):
                wait(dve, o_ready, HB * (b_ - 1))
                for k in range(HB):
                    ts = slice(k * TPB, (k + 1) * TPB)
                    dve.wait_ge(t2_done, HB * b_ + k + 1)
                    nc.vector.tensor_tensor(x1[:, par, ts], x_sb[:, par, ts], TR[k][:, :].rearrange("p (t d) -> p t d", d=D),
                                            ALU.add).then_inc(x1_ready, 1)
                for j in range(TT):
                    dve.wait_ge(x1_ready, HB * b_ + j // TPB + 1)
                    nc.vector.bn_stats(st2[:, j], x1[:, par, j]).then_inc(dve_st2, 1)
                used, full = snapped(dve, b_), snapped(dve, TT * (b_ + 1))
                dve.wait_ge(s_pool_const, 8)
                wait(dve, norm2_ready, used)
                dve.wait_ge(dve_st2, full)
                for j in range(TT):
                    ins = nc.vector.bn_aggr(mv2[:, j], st2[:, j])
                ins.then_inc(stats2_ready, 1)

            def scan(b_):
                wait(dve, mix_done, DC * b_)
                for c in range(DC):
                    dve.wait_ge(h_ready, DC * b_ + c + 1)
                    nc.vector.tensor_tensor_scan(S[:, c], keep[:, c:c + 1].to_broadcast([P, T]), h[:, c, PAD:PAD + T],
                                                 0.0, ALU.mult, ALU.add).then_inc(S_ready, 1)

            def slot(i, half, par):
                opp = 1 - par
                if inside(i, 1):
                    conv(i + 1)
                if inside(i, 0):
                    router(i, par)
                if inside(i, 2):
                    stats1(i + 2, half + 1, par)
                if inside(i, -1):
                    residual2(i - 1, half - 1 if par == 0 else half, opp)
                if inside(i, 1):
                    residual1(i + 1, opp)
                if inside(i, 2):
                    scan(i + 2)

            slots(dve, slot)

        @block.tensor
        def _(pe):
            mm = nc.tensor.matmul
            pe.wait_ge(s_pool_const, 8)
            pe.wait_ge(s_setup, SETUP_LOADED)
            for c in range(DC):
                ins = nc.tensor.transpose(Y[0][:, c * B:(c + 1) * B], c_nat[:, c * P:(c + 1) * P], ident[0:B, 0:B])
            ins.then_inc(s_pe_setup, 1)
            for d in range(DC):
                for e in range(DC):
                    ins = nc.tensor.transpose(Y[1][:, d * D + e * P:d * D + (e + 1) * P], w_nat[:, e, d * P:(d + 1) * P], ident[:, :])
            ins.then_inc(s_pe_setup, 1)
            pe.wait_ge(s_act_setup, 1 + DC)
            pe.wait_ge(s_wmod, 16)
            for g in range(5):
                for d in range(DC):
                    col = (g * DC + d) * B
                    for c in range(DC):
                        ins = mm(TR[0][:, col:col + B], wmod_sb[:, c, g * D + d * P:g * D + (d + 1) * P], silu_cT[:, c],
                                 start=(c == 0), stop=(c == DC - 1))
            ins.then_inc(s_pe_setup, 1)
            for c in range(DC):
                ins = mm(TR[1][0:B, 0:D], silu_cT[:, c], wmod_sb[:, c, 5 * D:6 * D], start=(c == 0), stop=(c == DC - 1))
            ins.then_inc(s_pe_setup, 1)
            for c in range(DC):
                ins = mm(U[0][0:E, 0:D], b2_all[:, c], wo[:, c], start=(c == 0), stop=(c == DC - 1))
            ins.then_inc(s_pe_setup, 1)
            pe.wait_ge(s_act_setup, 1 + 2 * DC)
            for e in range(E):
                pe.wait_ge(s_w2[e % 2], 16 * (e // 2 + 1))
                wait(pe, s_w2T_cp, DC * e)
                for c in range(DC):
                    for f in range(FC):
                        ins = nc.tensor.transpose(Y[c][:, f * P:(f + 1) * P], w2_nat[:, e % 2, f, c * P:(c + 1) * P], ident[:, :])
                ins.then_inc(s_w2T_mm, 1)
                pe.wait_ge(s_w2T_cp, DC * (e + 1))
                wait(pe, s_pack, 2 * e)
                for k in range(2):
                    for f in range(FC // 2):
                        fk = k * FC // 2 + f
                        for c in range(DC):
                            ins = mm(Q[k][:, f * D:(f + 1) * D], w2T[:, e % 2, c, fk * P:(fk + 1) * P], wo[:, c],
                                     start=(c == 0), stop=(c == DC - 1))
                    ins.then_inc(s_comb, 1)
            pe.wait_ge(s_pack, 2 * E)
            pe.wait_ge(s_dve_setup, SETUP_STEPS)

            def down(b_, par, k):
                for t in range(TPB):
                    j = k * TPB + t
                    tj = slice(j * P, (j + 1) * P)
                    cols = Q[k][:, t * D:(t + 1) * D]
                    mm(cols, ones_r[:, :], beta_w[:, par], start=True, stop=False)
                    for c in range(DC):
                        mm(Q[k][:, t * D + c * P:t * D + (c + 1) * P], hid[:, par, c, tj], ident[:, :], start=False, stop=False)
                    for f in range(FC):
                        ins = mm(cols, hg[:, f, tj], down_w[:, par, f * D:(f + 1) * D], start=False, stop=(f == FC - 1))
                ins.then_inc(down_done, 1)

            def slot(i, half, par):
                opp = 1 - par
                if inside(i, 1):
                    pe.wait_ge(S_ready, DC * (i + 2))
                    for e in range(DC):
                        for d in range(DC):
                            ins = mm(Y[e][:, :], mixT[:, d, e * P:(e + 1) * P], S[:, d], start=(d == 0), stop=(d == DC - 1))
                        ins.then_inc(mix_done, 1)
                if inside(i, 0):
                    pe.wait_ge(hid_ready, DC * (i + 1))
                    for c in range(DC):
                        ins = mm(TR[0][:, 0:1], wp1[:, c], hid[:, par, c, T - 1:T], start=(c == 0), stop=(c == DC - 1))
                    ins.then_inc(r_nav, 1)
                if inside(i, -1):
                    pe.wait_ge(gelu_ready, FC * i)
                    wait(pe, scaled, HB * (i - 2) + HB)
                    down(i - 1, opp, 0)
                if inside(i, 0):
                    pe.wait_ge(nav_ready, i + 1)
                    mm(TR[0][0:1, 8:8 + E], nav[:, :], wp2[:, :], start=True, stop=True).then_inc(r_logits, 1)
                if inside(i, -1):
                    down(i - 1, opp, 1)
                if inside(i, 1):
                    wait(pe, sel_ready, i + 1)
                    pe.wait_ge(r1_ready, DC * (i + 2))
                    for k in range(HB):
                        for t in range(TPB):
                            j = k * TPB + t
                            for c in range(DC):
                                ins = nc.tensor.transpose(TR[k][:, t * D + c * P:t * D + (c + 1) * P],
                                                          r1T[:, c, j * P:(j + 1) * P], ident[:, :])
                        ins.then_inc(t2_done, 1)
                if inside(i, 2):
                    wait(pe, r1_ready, DC * (i + 2))
                    for c in range(DC):
                        for j in range(TT):
                            pe.wait_ge(xn1_ready, TT * (i + 2) + j + 1)
                            ins = nc.tensor.transpose(Y[c][:, j * P:(j + 1) * P], xn1[:, j, c * P:(c + 1) * P], ident[:, :])
                        ins.then_inc(t1_done, 1)
                if inside(i, 0):
                    pe.wait_ge(w_loaded[par], 48 * (half + 1))
                    for f in range(FC):
                        wait(pe, gelu_ready, FC * i + f - 1)
                        for c in range(DC):
                            ins = mm(U[f % 2][:, :], up_w[:, par, c, f * P:(f + 1) * P], hid[:, par, c], start=(c == 0), stop=(c == DC - 1))
                        ins.then_inc(up_done, 1)
                if inside(i, 1):
                    for c in range(DC):
                        for j in range(TT):
                            pe.wait_ge(xn2_ready, TT * (i + 1) + j + 1)
                            ins = nc.tensor.transpose(TR[c][:, j * P:(j + 1) * P], xn2[:, j, c * P:(c + 1) * P], ident[:, :])
                        ins.then_inc(t3_done, 1)

            slots(pe, slot)


_INS = ['L0_attn_x', 'L0_attn_decay_logit', 'L0_attn_W', 'L0_attn_b', 'L0_attn_conv_w', 'L0_attn_conv_b',
        'L0_ffn_Wp1', 'L0_ffn_bp1', 'L0_ffn_Wp2', 'L0_ffn_bp2', 'L0_ffn_W1', 'L0_ffn_b1', 'L0_ffn_W2', 'L0_ffn_b2',
        'L0_ffn_Wo', 'L0_ffn_bo', 'L0_c', 'L0_wmod']
_OUTS = [((32, 512, 256), 'float32')]


def kernel(**inputs):
    import numpy as _np
    import concourse.bacc as _bacc
    from concourse import mybir as _mybir
    from concourse.bass_utils import run_bass_kernel_spmd as _run

    nc = _bacc.Bacc("TRN2", target_bir_lowering=False, num_devices=1)
    arrays, args = {}, []
    for name in _INS:
        a = _np.ascontiguousarray(inputs[name])
        arrays[f"in_{name}_dram"] = a
        args.append(nc.dram_tensor(f"in_{name}_dram", a.shape, _mybir.dt.from_np(a.dtype), kind="ExternalInput").ap())
    for i, (shape, dtype) in enumerate(_OUTS):
        dt = _mybir.dt.from_np(_np.dtype(dtype))
        args.append(nc.dram_tensor(f"out_{i}_dram", shape, dt, kind="ExternalOutput").ap())
    adaln_attention_ffn_kernel(nc, *args)
    r = _run(nc, [arrays], core_ids=[0])
    got = tuple(r.results[0][f"out_{i}_dram"] for i in range(len(_OUTS)))
    return got[0]
```

```python
import concourse.bass as bass
from concourse import mybir
from contextlib import ExitStack


def adaln_attention_ffn_kernel(nc, x, decay_logit, W, b, conv_w, conv_b, Wp1, bp1, Wp2, bp2,
                               W1, b1, W2, b2, Wo, bo, c_in, wmod, out):
    f32 = mybir.dt.float32
    f32r = mybir.dt.float32r
    u32 = mybir.dt.uint32
    ALU = mybir.AluOpType
    ACT = mybir.ActivationFunctionType

    P = 128
    B, T, D = x.shape
    E, _, F = W1.shape
    NAV = Wp1.shape[1]
    TAPS = conv_w.shape[2]
    PAD = (TAPS - 1) // 2
    TT = T // P
    DC = D // P
    FC = F // P
    TPB = 512 // D
    HB = TT // TPB
    CONV_HEAD = 3
    EPS = 1e-5
    OUT_SCALE = 0.3
    GATE_MIN = 0.25
    CA, SA, GA, GAB, CB, SB = (DC * n for n in range(6))
    MODS = 6 * DC
    UP = DC * F
    DOWN = FC * D
    UP_PACK = 2 * UP + FC

    up_table = nc.dram_tensor("up_table", (E, P, UP_PACK), f32, kind="Internal").ap()
    down_table = nc.dram_tensor("down_table", (E, P, 2 * DOWN), f32, kind="Internal").ap()
    beta_table = nc.dram_tensor("beta_table", (E, 2, D), f32, kind="Internal").ap()
    gate_table = nc.dram_tensor("gate_table", (B, D), f32, kind="Internal").ap()

    def tok(dram):
        return dram.rearrange("(t p) d -> p t d", p=P)

    with ExitStack() as ctx:
        def sb(name, shape, dt=f32):
            return ctx.enter_context(nc.sbuf_tensor(name, shape, dt))

        def bank(name):
            return ctx.enter_context(nc.psum_tensor(name, [P, 512], f32))

        def sem(name):
            return ctx.enter_context(nc.semaphore(name))

        ident = sb("ident", [P, P])
        ident_r = sb("ident_r", [P, P], f32r)
        ones_r = sb("ones_r", [P, P], f32r)
        decay = sb("decay", [P, DC])
        keep = sb("keep", [P, DC])
        fresh = sb("fresh", [P, DC])
        w_nat = sb("w_nat", [P, DC, D])
        mixT = sb("mixT", [P, DC, D])
        taps = sb("taps", [P, DC, TAPS])
        bias_b = sb("bias_b", [P, DC])
        bias_c = sb("bias_c", [P, DC])
        bias_bc = sb("bias_bc", [P, DC])
        wp1 = sb("wp1", [P, DC, NAV])
        bp1_sb = sb("bp1_sb", [P, 1])
        wp2 = sb("wp2", [P, E])
        bp2_sb = sb("bp2_sb", [1, E])
        wo = sb("wo", [P, DC, D])
        b1_all = sb("b1_all", [P, E, FC])
        b2_all = sb("b2_all", [P, DC, E])
        bo_all = sb("bo_all", [E, D])
        c_nat = sb("c_nat", [B, D])
        silu_cT = sb("silu_cT", [P, DC, B])
        wmod_sb = sb("wmod_sb", [P, DC, 6 * D])
        mods = sb("mods", [P, B, MODS])
        gate_raw = sb("gate_raw", [P, DC, B])
        gate_sign = sb("gate_sign", [P, DC, B])
        gate_size = sb("gate_size", [P, DC, B])
        gate = sb("gate", [P, DC, B])
        gb_raw = sb("gb_raw", [B, D])
        gb_sign = sb("gb_sign", [B, D])
        gb_size = sb("gb_size", [B, D])
        gb_rows = sb("gb_rows", [B, D])
        beta = sb("beta", [E, D])
        beta3 = sb("beta3", [E, D])
        beta_parts = sb("beta_parts", [E, 2, D], f32r)
        w1_nat = sb("w1_nat", [P, 2, UP])
        w2_nat = sb("w2_nat", [P, 2, FC, D])
        w2T = sb("w2T", [P, DC, F])
        eps_t = sb("eps_t", [P, TT])
        minus_half = sb("minus_half", [P, TT])
        minus_one = sb("minus_one", [P, TT])

        x_sb = sb("x_sb", [P, 2, TT, D])
        modc = sb("modc", [P, 2, MODS])
        st1 = sb("st1", [P, TT, 6])
        mv1 = sb("mv1", [P, TT, 2])
        ve1 = sb("ve1", [P, TT])
        rstd1 = sb("rstd1", [P, TT])
        mr1 = sb("mr1", [P, TT])
        nmr1 = sb("nmr1", [P, TT])
        xn1 = sb("xn1", [P, TT, D])
        h = sb("h", [P, DC, T + 2 * PAD])
        S = sb("S", [P, DC, T])
        r1T = sb("r1T", [P, DC, T])
        x1 = sb("x1", [P, 2, TT, D])
        st2 = sb("st2", [P, TT, 6])
        mv2 = sb("mv2", [P, TT, 2])
        ve2 = sb("ve2", [P, TT])
        rstd2 = sb("rstd2", [P, TT])
        mr2 = sb("mr2", [P, TT])
        nmr2 = sb("nmr2", [P, TT])
        xn2 = sb("xn2", [P, TT, D])
        hid = sb("hid", [P, DC, T])
        hid_hi = sb("hid_hi", [P, 2, DC, T], f32r)
        hid_lo = sb("hid_lo", [P, 2, DC, T], f32r)
        nav = sb("nav", [P, 1])
        logits = sb("logits", [1, E])
        top8 = sb("top8", [1, 8])
        sel8 = sb("sel8", [1, 2, 8], u32)
        up_w = sb("up_w", [P, 2, UP_PACK], f32r)
        down_w = sb("down_w", [P, 2, 2 * DOWN], f32r)
        beta_w = sb("beta_w", [P, 2, D], f32r)
        g = sb("g", [P, FC, T])
        g_hi = sb("g_hi", [P, FC, T], f32r)
        g_lo = sb("g_lo", [P, FC, T], f32r)
        gb_bc = sb("gb_bc", [P, 2, D])
        o_sb = sb("o_sb", [P, 2, TT, D])

        Y = [bank("Y0"), bank("Y1")]
        TR = [bank("TR0"), bank("TR1")]
        U = [bank("U0"), bank("U1")]
        Q = [bank("Q0"), bank("Q1")]

        s_setup = sem("s_setup")
        s_wmod = sem("s_wmod")
        s_w2 = [sem("s_w2a"), sem("s_w2b")]
        s_pool_const = sem("s_pool_const")
        s_pe_setup = sem("s_pe_setup")
        s_act_setup = sem("s_act_setup")
        s_dve_setup = sem("s_dve_setup")
        s_tables = sem("s_tables")
        s_w1 = [sem("s_w1a"), sem("s_w1b")]
        s_ident_r = sem("s_ident_r")
        s_w2T_mm = sem("s_w2T_mm")
        s_w2T_cp = sem("s_w2T_cp")
        s_comb = sem("s_comb")
        s_up_hi = sem("s_up_hi")
        s_up_lo = sem("s_up_lo")
        s_down_hi = sem("s_down_hi")
        s_down_lo = sem("s_down_lo")
        s_saved = [sem("s_saved0"), sem("s_saved1")]

        x_loaded = [sem("x_loaded0"), sem("x_loaded1")]
        gb_loaded = [sem("gb_loaded0"), sem("gb_loaded1")]
        up_loaded = [sem("up_loaded0"), sem("up_loaded1")]
        down_loaded = [sem("down_loaded0"), sem("down_loaded1")]
        stored = [sem("stored0"), sem("stored1")]
        modc_ready = sem("modc_ready")
        dve_st1 = sem("dve_st1")
        stats1_ready = sem("stats1_ready")
        pool_rstd1 = sem("pool_rstd1")
        norm1_ready = sem("norm1_ready")
        xn1_ready = sem("xn1_ready")
        t1_done = sem("t1_done")
        h_ready = sem("h_ready")
        S_ready = sem("S_ready")
        mix_done = sem("mix_done")
        conv_step = sem("conv_step")
        conv_done = sem("conv_done")
        r1_ready = sem("r1_ready")
        t2_done = sem("t2_done")
        x1_ready = sem("x1_ready")
        dve_st2 = sem("dve_st2")
        stats2_ready = sem("stats2_ready")
        pool_rstd2 = sem("pool_rstd2")
        norm2_ready = sem("norm2_ready")
        xn2_ready = sem("xn2_ready")
        t3_done = sem("t3_done")
        hid_ready = sem("hid_ready")
        r_nav = sem("r_nav")
        nav_ready = sem("nav_ready")
        r_logits = sem("r_logits")
        dve_router = sem("dve_router")
        sel_ready = sem("sel_ready")
        up_done = sem("up_done")
        gelu_out = sem("gelu_out")
        g_hi_ready = sem("g_hi_ready")
        g_lo_ready = sem("g_lo_ready")
        hid_hi_ready = sem("hid_hi_ready")
        hid_lo_ready = sem("hid_lo_ready")
        down_done = sem("down_done")
        scaled = sem("scaled")
        o_ready = sem("o_ready")

        SETUP_LOADED = 16 * (12 + E + DC)
        GATES_DONE = 16
        SETUP_STEPS = GATES_DONE + 2 * DC + 4

        EXPERTS_AT = {(-3, "start"): (0, 1, 2), (-2, "middle"): (3,), (-2, "end"): (4,),
                      (-1, "start"): (5,), (-1, "middle"): (6,), (-1, "end"): (7,)}

        def experts_at(i, place):
            return EXPERTS_AT.get((i, place), ()) if isinstance(i, int) else ()

        def wait(eng, s, v):
            if not isinstance(v, int) or v > 0:
                eng.wait_ge(s, v)

        def snapped(eng, v):
            return v if isinstance(v, int) else eng.snap(eng.to_reg(v), min_val=0, max_val=4096)

        def slots(eng, slot):
            for i in range(-3, 4):
                slot(i, i // 2, i % 2)
            with eng.Fori(2, B // 2 - 2) as m:
                slot(2 * m, m, 0)
                slot(2 * m + 1, m, 1)
            for i in range(B - 4, B + 1):
                slot(i, i // 2, i % 2)

        def inside(i, off):
            return not isinstance(i, int) or 0 <= i + off < B

        block = ctx.enter_context(nc.Block())

        @block.sync
        def _(sp):
            def load_x(i, half, par):
                wait(sp, x1_ready, 2 * (i - 1))
                sp.dma_start(x_sb[:, par], tok(x[bass.ds(i, 1)].rearrange("o t d -> (o t) d"))).then_inc(x_loaded[par], 16)

            load_x(0, 0, 0)
            load_x(1, 0, 1)
            small = [(decay[:, :], decay_logit.rearrange("(c p) -> p c", p=P)),
                     (w_nat[:, :, :], W.rearrange("(c p) d -> p c d", p=P)),
                     (c_nat[:, :], c_in),
                     (taps[:, :, :], conv_w.rearrange("(c p) o k -> p c (o k)", p=P)),
                     (bias_b[:, :], b.rearrange("(c p) -> p c", p=P)),
                     (bias_c[:, :], conv_b.rearrange("(c p) -> p c", p=P)),
                     (wp1[:, :, :], Wp1.rearrange("(c p) n -> p c n", p=P)),
                     (bp1_sb[:, :], bp1.rearrange("(p o) -> p o", o=1)),
                     (wp2[:, :], Wp2),
                     (bp2_sb[:, :], bp2.rearrange("(o e) -> o e", o=1)),
                     (wo[:, :, :], Wo.rearrange("(c p) d -> p c d", p=P)),
                     (bo_all[:, :], bo.rearrange("(o d) -> o d", o=1).to_broadcast([E, D]))]
            with nc.allow_non_contiguous_dma(reason="small vectors onto partitions"):
                for dst, src in small:
                    sp.dma_start(dst, src).then_inc(s_setup, 16)
                for e in range(E):
                    sp.dma_start(b1_all[:, e, :], b1[e].rearrange("(c p) -> p c", p=P)).then_inc(s_setup, 16)
                for c in range(DC):
                    sp.dma_start(b2_all[:, c, :], b2[:, c * P:(c + 1) * P].rearrange("e p -> p e")).then_inc(s_setup, 16)
            sp.dma_start(wmod_sb[:, :, :], wmod.rearrange("(c p) n -> p c n", p=P)).then_inc(s_wmod, 16)

            for e in range(E + 1):
                if e < E:
                    wait(sp, s_w2T_mm, e - 1)
                    sp.dma_start(w2_nat[:, e % 2], W2[e].rearrange("(c p) d -> p c d", p=P)).then_inc(s_w2[e % 2], 16)
                    wait(sp, s_up_lo, e - 1)
                    sp.dma_start(w1_nat[:, e % 2].rearrange("p (c f) -> p c f", c=DC),
                                 W1[e].rearrange("(c p) f -> p c f", p=P)).then_inc(s_w1[e % 2], 16)
                if e == E - 1:
                    load_x(2, 1, 0)
                if e >= 1:
                    q = (e - 1) % 2
                    sp.wait_ge(s_up_lo, e)
                    sp.dma_start(up_table[e - 1, :, 0:2 * UP], up_w[:, q, 0:2 * UP].bitcast(f32)).then_inc(s_saved[q], 16)
                    sp.wait_ge(s_down_lo, 2 * e)
                    sp.dma_start(down_table[e - 1], down_w[:, q].bitcast(f32)).then_inc(s_saved[q], 16)
            with nc.allow_non_contiguous_dma(reason="up biases behind the up weights"):
                sp.dma_start(up_table[:, :, 2 * UP:UP_PACK].rearrange("e p f -> p e f"), b1_all[:, :, :]).then_inc(s_tables, 16)
            sp.wait_ge(s_dve_setup, SETUP_STEPS)
            sp.dma_start(gate_table, gb_rows[:, :]).then_inc(s_tables, 16)
            sp.dma_start(beta_table, beta_parts[:, :, :].bitcast(f32)).then_inc(s_tables, 16)
            sp.wait_ge(s_tables, 48)
            for q in s_saved:
                sp.wait_ge(q, 16 * E)

            def slot(i, half, par):
                if inside(i, 0):
                    used, chosen = snapped(sp, HB * (i - 1)), snapped(sp, i + 1)
                    sp.wait_ge(s_setup, SETUP_LOADED)
                    wait(sp, down_done, used)
                    sp.wait_ge(sel_ready, chosen)
                    e = sp.value_load(sel8[0:1, par, 0:1], min_val=0, max_val=E - 1)
                    sp.dma_start(up_w[:, par].bitcast(f32), up_table[bass.ds(e, 1)].rearrange("o p n -> p (o n)")).then_inc(up_loaded[par], 16)
                    sp.dma_start(down_w[:, par].bitcast(f32), down_table[bass.ds(e, 1)].rearrange("o p n -> p (o n)")).then_inc(down_loaded[par], 16)
                    sp.dma_start(beta_w[0:2, par].bitcast(f32), beta_table[bass.ds(e, 1)].rearrange("o k d -> (o k) d")).then_inc(down_loaded[par], 16)
                if inside(i, -1):
                    for k in range(HB):
                        sp.wait_ge(o_ready, HB * (i - 1) + k + 1)
                        ts = slice(k * TPB, (k + 1) * TPB)
                        sp.dma_start(tok(out[bass.ds(i - 1, 1)].rearrange("o t d -> (o t) d"))[:, ts], o_sb[:, 1 - par, ts]).then_inc(stored[1 - par], 16)
                if inside(i, 1):
                    wait(sp, scaled, HB * i)
                    sp.dma_start(gb_bc[:, 1 - par], gate_table[bass.ds(i + 1, 1)].to_broadcast([P, D])).then_inc(gb_loaded[1 - par], 16)
                if inside(i, 3) and inside(i, 0):
                    load_x(i + 3, half + 1, 1 - par)

            slots(sp, slot)
            for q in stored:
                sp.wait_ge(q, 16 * HB * B // 2)

        @block.gpsimd
        def _(pool):
            nc.gpsimd.memset(ident[:, :], 0.0).then_inc(s_pool_const, 1)
            nc.gpsimd.memset(eps_t[:, :], EPS).then_inc(s_pool_const, 1)
            nc.gpsimd.memset(minus_half[:, :], -0.5).then_inc(s_pool_const, 1)
            nc.gpsimd.memset(minus_one[:, :], -1.0).then_inc(s_pool_const, 1)
            nc.gpsimd.memset(ones_r[:, :].bitcast(f32), 1.0).then_inc(s_pool_const, 1)
            nc.gpsimd.memset(beta_w[:, :, :].bitcast(f32), 0.0).then_inc(s_pool_const, 1)
            nc.gpsimd.memset(h[:, :, :], 0.0).then_inc(s_pool_const, 1)
            pool.wait_ge(s_pool_const, 7)
            nc.gpsimd.affine_select(out=ident[:, :], in_=ident[:, :], compare_op=ALU.not_equal, fill=1.0,
                                    base=0, pattern=[[-1, P]], channel_multiplier=1).then_inc(s_pool_const, 1)

            def norm_scale(b_, stats_ready, consumed, mv, ve, rstd, mr, nmr, steps, ready):
                pool.wait_ge(stats_ready, b_ + 1)
                wait(pool, consumed, TT * b_)
                nc.gpsimd.tensor_tensor(ve[:, :], mv[:, :, 1], eps_t[:, :], ALU.add).then_inc(steps, 1)
                pool.wait_ge(steps, 3 * b_ + 1)
                nc.gpsimd.tensor_tensor(rstd[:, :], ve[:, :], minus_half[:, :], ALU.pow).then_inc(steps, 1)
                pool.wait_ge(steps, 3 * b_ + 2)
                nc.gpsimd.tensor_tensor(mr[:, :], mv[:, :, 0], rstd[:, :], ALU.mult).then_inc(steps, 1)
                pool.wait_ge(steps, 3 * b_ + 3)
                nc.gpsimd.tensor_tensor(nmr[:, :], mr[:, :], minus_one[:, :], ALU.mult).then_inc(ready, 1)

            def slot(i, half, par):
                opp = 1 - par
                if inside(i, 0):
                    wait(pool, down_done, HB * (i - 1))
                    for c in range(DC):
                        pool.wait_ge(hid_hi_ready, DC * i + c + 1)
                        nc.gpsimd.tensor_tensor(hid_lo[:, par, c], hid[:, c], hid_hi[:, par, c].bitcast(f32),
                                                ALU.subtract).then_inc(hid_lo_ready, 1)

                if inside(i, 1):
                    norm_scale(i + 1, stats2_ready, xn2_ready, mv2, ve2, rstd2, mr2, nmr2, pool_rstd2, norm2_ready)
                if inside(i, 0):
                    wait(pool, down_done, HB * i)
                    for f in range(FC):
                        pool.wait_ge(g_hi_ready, FC * i + f + 1)
                        nc.gpsimd.tensor_tensor(g_lo[:, f], g[:, f], g_hi[:, f].bitcast(f32), ALU.subtract).then_inc(g_lo_ready, 1)
                if inside(i, 3):
                    norm_scale(i + 3, stats1_ready, xn1_ready, mv1, ve1, rstd1, mr1, nmr1, pool_rstd1, norm1_ready)

            slots(pool, slot)

        @block.scalar
        def _(act):
            act.wait_ge(s_setup, SETUP_LOADED)
            nc.scalar.activation(keep[:, :], decay[:, :], ACT.Sigmoid).then_inc(s_act_setup, 1)
            act.wait_ge(s_pe_setup, 1)
            for c in range(DC):
                nc.scalar.activation(silu_cT[:, c], Y[0][:, c * B:(c + 1) * B], ACT.Silu).then_inc(s_act_setup, 1)
            act.wait_ge(s_dve_setup, 1)
            act.wait_ge(s_pe_setup, 2)
            for c in range(DC):
                nc.scalar.activation(mixT[:, c], Y[1][:, c * D:(c + 1) * D], ACT.Copy,
                                     scale=fresh[:, c:c + 1]).then_inc(s_act_setup, 1)
            def expert(e):
                act.wait_ge(s_w1[e % 2], 16 * (e // 2 + 1))
                wait(act, s_saved[e % 2], 32 * (e // 2))
                nc.scalar.copy(up_w[:, e % 2, 0:UP], w1_nat[:, e % 2]).then_inc(s_up_hi, 1)
                for k in range(2):
                    act.wait_ge(s_comb, 2 * e + k + 1)
                    nc.scalar.activation(down_w[:, e % 2, k * DOWN // 2:(k + 1) * DOWN // 2], Q[k][:, :], ACT.Copy,
                                         scale=OUT_SCALE).then_inc(s_down_hi, 1)

            def normalise(b_, src, dst, rstd, nmr, scale_ready, used, ready):
                act.wait_ge(scale_ready, b_ + 1)
                wait(act, used, DC * b_)
                for j in range(TT):
                    nc.scalar.activation(dst[:, j], src[:, j], ACT.Identity, bias=nmr[:, j:j + 1],
                                         scale=rstd[:, j:j + 1]).then_inc(ready, 1)

            def slot(i, half, par):
                opp = 1 - par
                for e in experts_at(i, "start"):
                    expert(e)
                if inside(i, 0):
                    act.wait_ge(r_nav, i + 1)
                    nc.scalar.activation(nav[:, :], TR[0][:, 0:1], ACT.Gelu, bias=bp1_sb[:, 0:1]).then_inc(nav_ready, 1)
                if inside(i, 2):
                    normalise(i + 2, x_sb[:, par], xn1, rstd1, nmr1, norm1_ready, t1_done, xn1_ready)
                if inside(i, 1):
                    wait(act, t2_done, HB * (i + 1))
                    for c in range(DC):
                        act.wait_ge(conv_done, DC * (i + 1) + c + 1)
                        nc.scalar.activation(r1T[:, c], Y[c][:, :], ACT.Identity, bias=modc[:, opp, GAB + c:GAB + c + 1],
                                             scale=modc[:, opp, GA + c:GA + c + 1]).then_inc(r1_ready, 1)
                if inside(i, 2):
                    wait(act, conv_done, DC * (i + 2))
                    act.wait_ge(modc_ready, i + 3)
                    for c in range(DC):
                        act.wait_ge(t1_done, DC * (i + 2) + c + 1)
                        nc.scalar.activation(h[:, c, PAD:PAD + T], Y[c][:, :], ACT.Identity, bias=modc[:, par, SA + c:SA + c + 1],
                                             scale=modc[:, par, CA + c:CA + c + 1]).then_inc(h_ready, 1)
                for e in experts_at(i, "middle"):
                    expert(e)

                def gelu(f):
                    act.wait_ge(up_done, FC * i + f + 1)
                    nc.scalar.activation(g[:, f], U[f % 2][:, :], ACT.Gelu,
                                         bias=up_w[:, par, 2 * UP + f:2 * UP + f + 1].bitcast(f32)).then_inc(gelu_out, 1)

                def high(f):
                    act.wait_ge(gelu_out, FC * i + f + 1)
                    nc.scalar.copy(g_hi[:, f], g[:, f]).then_inc(g_hi_ready, 1)

                if inside(i, 0):
                    act.wait_ge(up_loaded[par], 16 * (half + 1))
                    wait(act, down_done, HB * i)
                    gelu(0)
                    high(0)
                    gelu(1)
                    high(1)
                    gelu(2)
                    high(2)
                if inside(i, 1):
                    normalise(i + 1, x1[:, opp], xn2, rstd2, nmr2, norm2_ready, t3_done, xn2_ready)
                if inside(i, 0):
                    gelu(3)
                    high(3)
                for e in experts_at(i, "end"):
                    expert(e)
                if inside(i, 1):
                    wait(act, hid_lo_ready, DC * (i + 1))
                    wait(act, r_nav, i + 1)
                    wait(act, down_done, HB * i)
                    for c in range(DC):
                        act.wait_ge(t3_done, DC * (i + 1) + c + 1)
                        nc.scalar.activation(hid[:, c], TR[c][:, :], ACT.Identity, bias=modc[:, opp, SB + c:SB + c + 1],
                                             scale=modc[:, opp, CB + c:CB + c + 1]).then_inc(hid_ready, 1)
                    for c in range(DC):
                        act.wait_ge(hid_ready, DC * (i + 1) + c + 1)
                        nc.scalar.copy(hid_hi[:, opp, c], hid[:, c]).then_inc(hid_hi_ready, 1)

            slots(act, slot)

        @block.vector
        def _(dve):
            step = [0]

            def done(ins):
                ins.then_inc(s_dve_setup, 1)
                step[0] += 1
                return step[0]

            dve.wait_ge(s_act_setup, 1)
            done(nc.vector.tensor_scalar(fresh[:, :], keep[:, :], -1.0, 1.0, ALU.mult, ALU.add))
            dve.wait_ge(s_setup, SETUP_LOADED)
            n = done(nc.vector.tensor_tensor(bias_bc[:, :], bias_b[:, :], bias_c[:, :], ALU.add))

            dve.wait_ge(s_pe_setup, 3)
            view = TR[0][:, 0:5 * DC * B].rearrange("p (g c r) -> p g c r", g=5, c=DC)
            m4 = mods[:, :, :].rearrange("p r (g c) -> p g c r", c=DC)
            done(nc.vector.tensor_copy(m4[:, SA // DC], view[:, 0]))
            done(nc.vector.tensor_scalar_add(m4[:, CA // DC], view[:, 1], 1.0))
            done(nc.vector.tensor_copy(m4[:, SB // DC], view[:, 3]))
            done(nc.vector.tensor_scalar_add(m4[:, CB // DC], view[:, 4], 1.0))
            n = done(nc.vector.tensor_copy(gate_raw[:, :, :], view[:, 2]))
            dve.wait_ge(s_dve_setup, n)
            done(nc.vector.tensor_scalar(gate_sign[:, :, :], gate_raw[:, :, :], 0.0, 2.0, ALU.is_ge, ALU.mult))
            n = done(nc.vector.scalar_tensor_tensor(out=gate_size[:, :, :], in0=gate_raw[:, :, :], scalar=-1.0, in1=gate_raw[:, :, :], op0=ALU.mult, op1=ALU.max))
            dve.wait_ge(s_dve_setup, n)
            n = done(nc.vector.tensor_scalar_max(gate_size[:, :, :], gate_size[:, :, :], GATE_MIN))
            dve.wait_ge(s_dve_setup, n)
            n = done(nc.vector.scalar_tensor_tensor(out=gate[:, :, :], in0=gate_sign[:, :, :], scalar=-1.0,
                                                    in1=gate_size[:, :, :], op0=ALU.add, op1=ALU.mult))
            dve.wait_ge(s_pe_setup, 4)
            n = done(nc.vector.tensor_copy(gb_raw[:, :], TR[1][0:B, 0:D]))
            dve.wait_ge(s_dve_setup, n)
            done(nc.vector.tensor_scalar(gb_sign[:, :], gb_raw[:, :], 0.0, 2.0, ALU.is_ge, ALU.mult))
            n = done(nc.vector.scalar_tensor_tensor(out=gb_size[:, :], in0=gb_raw[:, :], scalar=-1.0, in1=gb_raw[:, :], op0=ALU.mult, op1=ALU.max))
            dve.wait_ge(s_dve_setup, n)
            n = done(nc.vector.tensor_scalar_max(gb_size[:, :], gb_size[:, :], GATE_MIN))
            dve.wait_ge(s_dve_setup, n)
            n = done(nc.vector.scalar_tensor_tensor(out=gb_rows[:, :], in0=gb_sign[:, :], scalar=-1.0,
                                                    in1=gb_size[:, :], op0=ALU.add, op1=ALU.mult))
            assert n == GATES_DONE
            for c in range(DC):
                done(nc.vector.tensor_copy(mods[:, :, GA + c], gate[:, c, :]))
                n = done(nc.vector.tensor_scalar(mods[:, :, GAB + c], gate[:, c, :], bias_bc[:, c:c + 1], None, ALU.mult))
            dve.wait_ge(s_pe_setup, 5)
            n = done(nc.vector.tensor_tensor(beta[:, :], U[0][0:E, 0:D], bo_all[:, :], ALU.add))
            dve.wait_ge(s_dve_setup, n)
            n = done(nc.vector.tensor_scalar_mul(beta3[:, :], beta[:, :], OUT_SCALE))
            dve.wait_ge(s_dve_setup, n)
            n = done(nc.vector.tensor_copy(beta_parts[:, 0, :], beta3[:, :]))
            dve.wait_ge(s_dve_setup, n)
            n = done(nc.vector.tensor_tensor(beta_parts[:, 1, :], beta3[:, :], beta_parts[:, 0, :].bitcast(f32), ALU.subtract))
            dve.wait_ge(s_dve_setup, n)
            assert n == SETUP_STEPS
            nc.vector.tensor_copy(ident_r[:, :], ident[:, :]).then_inc(s_ident_r, 1)

            def down_low(e):
                for k in range(2):
                    cols = slice(k * DOWN // 2, (k + 1) * DOWN // 2)
                    dve.wait_ge(s_down_hi, 2 * e + k + 1)
                    nc.vector.scalar_tensor_tensor(out=down_w[:, e % 2, DOWN + cols.start:DOWN + cols.stop], in0=Q[k][:, :],
                                                   scalar=OUT_SCALE, in1=down_w[:, e % 2, cols].bitcast(f32),
                                                   op0=ALU.mult, op1=ALU.subtract).then_inc(s_down_lo, 1)

            def expert(e):
                dve.wait_ge(s_w2T_mm, e + 1)
                wait(dve, s_comb, 2 * e)
                for c in range(DC):
                    nc.vector.tensor_copy(w2T[:, c], U[c][:, :]).then_inc(s_w2T_cp, 1)
                dve.wait_ge(s_up_hi, e + 1)
                nc.vector.tensor_tensor(up_w[:, e % 2, UP:2 * UP], w1_nat[:, e % 2], up_w[:, e % 2, 0:UP].bitcast(f32),
                                        ALU.subtract).then_inc(s_up_lo, 1)
                down_low(e)

            def conv(b_, k0, k1):
                for k in range(k0, k1):
                    for c in range(DC):
                        if k == 0:
                            dve.wait_ge(mix_done, DC * b_ + c + 1)
                        else:
                            dve.wait_ge(conv_step, (TAPS - 1) * DC * b_ + DC * (k - 1) + c + 1)
                        ins = nc.vector.scalar_tensor_tensor(out=Y[c][:, :], in0=h[:, c, k:k + T], scalar=taps[:, c, k:k + 1],
                                                             in1=Y[c][:, :], op0=ALU.mult, op1=ALU.add)
                        ins.then_inc(conv_step if k < TAPS - 1 else conv_done, 1)

            def router(b_, par):
                dve.wait_ge(r_logits, b_ + 1)
                nc.vector.tensor_tensor(logits[:, :], TR[0][0:1, 8:8 + E], bp2_sb[:, :], ALU.add).then_inc(dve_router, 1)
                count = snapped(dve, 2 * b_ + 1)
                dve.wait_ge(s_pool_const, 8)
                dve.wait_ge(dve_router, count)
                nc.vector.max(top8[:, :], logits[:, :]).then_inc(dve_router, 1)
                count = snapped(dve, 2 * b_ + 2)
                dve.wait_ge(s_pool_const, 8)
                dve.wait_ge(dve_router, count)
                nc.vector.max_index(sel8[:, par], top8[:, :], logits[:, :]).then_inc(sel_ready, 1)

            def residual2(b_, half, par, k):
                ts = slice(k * TPB, (k + 1) * TPB)
                if k == 0:
                    dve.wait_ge(gb_loaded[par], 16 * (half + 1))
                    wait(dve, stored[par], 16 * HB * half)
                dve.wait_ge(down_done, HB * b_ + k + 1)
                nc.vector.tensor_tensor(o_sb[:, par, ts], Q[k][:, :].rearrange("p (t d) -> p t d", d=D),
                                        gb_bc[:, par:par + 1].to_broadcast([P, TPB, D]), ALU.mult).then_inc(scaled, 1)
                dve.wait_ge(scaled, HB * b_ + k + 1)
                nc.vector.tensor_tensor(o_sb[:, par, ts], o_sb[:, par, ts], x1[:, par, ts], ALU.add).then_inc(o_ready, 1)

            def modulation(b_, par):
                wait(dve, hid_ready, DC * (b_ - 1))
                nc.vector.tensor_copy(modc[:, par:par + 1, :], mods[:, bass.ds(b_, 1), :]).then_inc(modc_ready, 1)

            def stats1(b_, half, par):
                dve.wait_ge(x_loaded[par], 16 * (half + 1))
                for j in range(TT):
                    nc.vector.bn_stats(st1[:, j], x_sb[:, par, j]).then_inc(dve_st1, 1)
                used, full = snapped(dve, b_), snapped(dve, TT * (b_ + 1))
                dve.wait_ge(s_pool_const, 8)
                wait(dve, norm1_ready, used)
                dve.wait_ge(dve_st1, full)
                for j in range(TT):
                    ins = nc.vector.bn_aggr(mv1[:, j], st1[:, j])
                ins.then_inc(stats1_ready, 1)

            def residual1(b_, par):
                wait(dve, o_ready, HB * (b_ - 1))
                for k in range(HB):
                    ts = slice(k * TPB, (k + 1) * TPB)
                    dve.wait_ge(t2_done, HB * b_ + k + 1)
                    nc.vector.tensor_tensor(x1[:, par, ts], x_sb[:, par, ts], TR[k][:, :].rearrange("p (t d) -> p t d", d=D),
                                            ALU.add).then_inc(x1_ready, 1)
                for j in range(TT):
                    dve.wait_ge(x1_ready, HB * b_ + j // TPB + 1)
                    nc.vector.bn_stats(st2[:, j], x1[:, par, j]).then_inc(dve_st2, 1)
                used, full = snapped(dve, b_), snapped(dve, TT * (b_ + 1))
                dve.wait_ge(s_pool_const, 8)
                wait(dve, norm2_ready, used)
                dve.wait_ge(dve_st2, full)
                for j in range(TT):
                    ins = nc.vector.bn_aggr(mv2[:, j], st2[:, j])
                ins.then_inc(stats2_ready, 1)

            def scan(b_):
                wait(dve, mix_done, DC * b_)
                for c in range(DC):
                    dve.wait_ge(h_ready, DC * b_ + c + 1)
                    nc.vector.tensor_tensor_scan(S[:, c], keep[:, c:c + 1].to_broadcast([P, T]), h[:, c, PAD:PAD + T],
                                                 0.0, ALU.mult, ALU.add).then_inc(S_ready, 1)

            def slot(i, half, par):
                opp = 1 - par
                for e in experts_at(i, "start"):
                    expert(e)
                if inside(i, 1):
                    conv(i + 1, 0, CONV_HEAD)
                if inside(i, 0):
                    router(i, par)
                if inside(i, 1):
                    conv(i + 1, CONV_HEAD, TAPS)
                if inside(i, 2):
                    modulation(i + 2, par)
                if inside(i, -1):
                    for k in range(HB):
                        residual2(i - 1, half - 1 if par == 0 else half, opp, k)
                if inside(i, 1):
                    residual1(i + 1, opp)
                for e in experts_at(i, "middle"):
                    expert(e)
                if inside(i, 2):
                    scan(i + 2)
                if inside(i, 3):
                    stats1(i + 3, half + 2 if par else half + 1, opp)
                for e in experts_at(i, "end"):
                    expert(e)

            slots(dve, slot)

        @block.tensor
        def _(pe):
            mm = nc.tensor.matmul
            pe.wait_ge(s_pool_const, 8)
            pe.wait_ge(s_setup, SETUP_LOADED)
            for c in range(DC):
                ins = nc.tensor.transpose(Y[0][:, c * B:(c + 1) * B], c_nat[:, c * P:(c + 1) * P], ident[0:B, 0:B])
            ins.then_inc(s_pe_setup, 1)
            for d in range(DC):
                for e in range(DC):
                    ins = nc.tensor.transpose(Y[1][:, d * D + e * P:d * D + (e + 1) * P], w_nat[:, e, d * P:(d + 1) * P], ident[:, :])
            ins.then_inc(s_pe_setup, 1)
            pe.wait_ge(s_act_setup, 1 + DC)
            pe.wait_ge(s_wmod, 16)
            for g in range(5):
                for d in range(DC):
                    col = (g * DC + d) * B
                    for c in range(DC):
                        ins = mm(TR[0][:, col:col + B], wmod_sb[:, c, g * D + d * P:g * D + (d + 1) * P], silu_cT[:, c],
                                 start=(c == 0), stop=(c == DC - 1))
            ins.then_inc(s_pe_setup, 1)
            for c in range(DC):
                ins = mm(TR[1][0:B, 0:D], silu_cT[:, c], wmod_sb[:, c, 5 * D:6 * D], start=(c == 0), stop=(c == DC - 1))
            ins.then_inc(s_pe_setup, 1)
            for c in range(DC):
                ins = mm(U[0][0:E, 0:D], b2_all[:, c], wo[:, c], start=(c == 0), stop=(c == DC - 1))
            ins.then_inc(s_pe_setup, 1)
            pe.wait_ge(s_act_setup, 1 + 2 * DC)
            pe.wait_ge(s_dve_setup, SETUP_STEPS)
            pe.wait_ge(s_ident_r, 1)

            def expert(e):
                pe.wait_ge(s_w2[e % 2], 16 * (e // 2 + 1))
                wait(pe, s_w2T_cp, DC * e)
                for c in range(DC):
                    for f in range(FC):
                        ins = nc.tensor.transpose(U[c][:, f * P:(f + 1) * P], w2_nat[:, e % 2, f, c * P:(c + 1) * P], ident[:, :])
                ins.then_inc(s_w2T_mm, 1)
                pe.wait_ge(s_w2T_cp, DC * (e + 1))
                wait(pe, s_down_lo, 2 * e)
                for k in range(2):
                    for f in range(FC // 2):
                        fk = k * FC // 2 + f
                        for c in range(DC):
                            ins = mm(Q[k][:, f * D:(f + 1) * D], w2T[:, c, fk * P:(fk + 1) * P], wo[:, c],
                                     start=(c == 0), stop=(c == DC - 1))
                    ins.then_inc(s_comb, 1)

            def three(out_, w_hi, w_lo, m_hi, m_lo, start, stop):
                mm(out_, w_lo, m_hi, start=start, stop=False)
                mm(out_, w_hi, m_lo, start=False, stop=False)
                return mm(out_, w_hi, m_hi, start=False, stop=stop)

            def down(b_, par, j):
                k, t = j // TPB, j % TPB
                tj = slice(j * P, (j + 1) * P)
                cols = Q[k][:, t * D:(t + 1) * D]
                mm(cols, ones_r[:, :], beta_w[:, par], start=True, stop=False)
                for c in range(DC):
                    for part in (hid_lo, hid_hi):
                        mm(Q[k][:, t * D + c * P:t * D + (c + 1) * P], part[:, par, c, tj], ident_r[:, :], start=False, stop=False)
                for f in range(FC):
                    ins = three(cols, g_hi[:, f, tj], g_lo[:, f, tj], down_w[:, par, f * D:(f + 1) * D],
                                down_w[:, par, DOWN + f * D:DOWN + (f + 1) * D], False, f == FC - 1)
                if t == TPB - 1:
                    ins.then_inc(down_done, 1)

            def slot(i, half, par):
                opp = 1 - par
                for e in experts_at(i, "start"):
                    expert(e)
                if inside(i, 0):
                    pe.wait_ge(hid_ready, DC * (i + 1))
                    for c in range(DC):
                        ins = mm(TR[0][:, 0:1], wp1[:, c], hid[:, c, T - 1:T], start=(c == 0), stop=(c == DC - 1))
                    ins.then_inc(r_nav, 1)
                if inside(i, -1):
                    pe.wait_ge(down_loaded[opp], 32 * (half if par == 0 else half + 1))
                    pe.wait_ge(g_lo_ready, FC * i)
                    wait(pe, scaled, HB * (i - 1))
                    down(i - 1, opp, 0)
                if inside(i, 0):
                    pe.wait_ge(nav_ready, i + 1)
                    mm(TR[0][0:1, 8:8 + E], nav[:, :], wp2[:, :], start=True, stop=True).then_inc(r_logits, 1)
                if inside(i, -1):
                    for j in range(1, TT):
                        down(i - 1, opp, j)
                if inside(i, 1):
                    wait(pe, sel_ready, i + 1)
                    pe.wait_ge(r1_ready, DC * (i + 2))
                    for k in range(HB):
                        for t in range(TPB):
                            j = k * TPB + t
                            for c in range(DC):
                                ins = nc.tensor.transpose(TR[k][:, t * D + c * P:t * D + (c + 1) * P],
                                                          r1T[:, c, j * P:(j + 1) * P], ident[:, :])
                        ins.then_inc(t2_done, 1)
                if inside(i, 2):
                    wait(pe, r1_ready, DC * (i + 2))
                    for c in range(DC):
                        for j in range(TT):
                            if c == 0:
                                pe.wait_ge(xn1_ready, TT * (i + 2) + j + 1)
                            ins = nc.tensor.transpose(Y[c][:, j * P:(j + 1) * P], xn1[:, j, c * P:(c + 1) * P], ident[:, :])
                        ins.then_inc(t1_done, 1)
                for e in experts_at(i, "middle"):
                    expert(e)
                if inside(i, 0):
                    pe.wait_ge(up_loaded[par], 16 * (half + 1))
                    pe.wait_ge(hid_lo_ready, DC * (i + 1))
                    for f in range(FC):
                        wait(pe, gelu_out, FC * i + f - 1)
                        for c in range(DC):
                            w = c * F + f * P
                            ins = three(U[f % 2][:, :], up_w[:, par, w:w + P], up_w[:, par, UP + w:UP + w + P],
                                        hid_hi[:, par, c], hid_lo[:, par, c], c == 0, c == DC - 1)
                        ins.then_inc(up_done, 1)
                for e in experts_at(i, "end"):
                    expert(e)

                def mix(e):
                    for d in range(DC):
                        ins = mm(Y[e][:, :], mixT[:, d, e * P:(e + 1) * P], S[:, d], start=(d == 0), stop=(d == DC - 1))
                    ins.then_inc(mix_done, 1)

                if inside(i, 2):
                    pe.wait_ge(S_ready, DC * (i + 3))
                    mix(0)
                if inside(i, 1):
                    for c in range(DC):
                        for j in range(TT):
                            if c == 0:
                                pe.wait_ge(xn2_ready, TT * (i + 1) + j + 1)
                            ins = nc.tensor.transpose(TR[c][:, j * P:(j + 1) * P], xn2[:, j, c * P:(c + 1) * P], ident[:, :])
                        ins.then_inc(t3_done, 1)
                if inside(i, 2):
                    mix(1)

            slots(pe, slot)


_INS = ['L0_attn_x', 'L0_attn_decay_logit', 'L0_attn_W', 'L0_attn_b', 'L0_attn_conv_w', 'L0_attn_conv_b',
        'L0_ffn_Wp1', 'L0_ffn_bp1', 'L0_ffn_Wp2', 'L0_ffn_bp2', 'L0_ffn_W1', 'L0_ffn_b1', 'L0_ffn_W2', 'L0_ffn_b2',
        'L0_ffn_Wo', 'L0_ffn_bo', 'L0_c', 'L0_wmod']
_OUTS = [((32, 512, 256), 'float32')]


def kernel(**inputs):
    import numpy as _np
    import concourse.bacc as _bacc
    from concourse import mybir as _mybir
    from concourse.bass_utils import run_bass_kernel_spmd as _run

    nc = _bacc.Bacc("TRN2", target_bir_lowering=False, num_devices=1)
    arrays, args = {}, []
    for name in _INS:
        a = _np.ascontiguousarray(inputs[name])
        arrays[f"in_{name}_dram"] = a
        args.append(nc.dram_tensor(f"in_{name}_dram", a.shape, _mybir.dt.from_np(a.dtype), kind="ExternalInput").ap())
    for i, (shape, dtype) in enumerate(_OUTS):
        dt = _mybir.dt.from_np(_np.dtype(dtype))
        args.append(nc.dram_tensor(f"out_{i}_dram", shape, dt, kind="ExternalOutput").ap())
    adaln_attention_ffn_kernel(nc, *args)
    r = _run(nc, [arrays], core_ids=[0])
    got = tuple(r.results[0][f"out_{i}_dram"] for i in range(len(_OUTS)))
    return got[0]
```

```python
import concourse.bass as bass
from concourse import mybir
from contextlib import ExitStack


def adaln_attention_ffn_kernel(nc, x, decay_logit, W, b, conv_w, conv_b, Wp1, bp1, Wp2, bp2,
                               W1, b1, W2, b2, Wo, bo, c_in, wmod, out):
    f32 = mybir.dt.float32
    f32r = mybir.dt.float32r
    u32 = mybir.dt.uint32
    ALU = mybir.AluOpType
    ACT = mybir.ActivationFunctionType

    P = 128
    B, T, D = x.shape
    E, _, F = W1.shape
    NAV = Wp1.shape[1]
    TAPS = conv_w.shape[2]
    PAD = (TAPS - 1) // 2
    TT = T // P
    DC = D // P
    FC = F // P
    TPB = 512 // D
    HB = TT // TPB
    CONV_HEAD = 6
    CONV_MID = 1
    DOWN_HEAD = 2
    GELU_HEAD = 2
    UNROLL = 4
    EPS = 1e-5
    OUT_SCALE = 0.3
    GATE_MIN = 0.25
    CA, SA, GA, GAB, CB, SB = (DC * n for n in range(6))
    MODS = 6 * DC
    UP = DC * F
    DOWN = FC * D
    V_DECAY, V_B, V_CONV, V_B1 = 0, DC, 2 * DC, 3 * DC
    V_B2 = V_B1 + E * FC
    V_BP1 = V_B2 + E * DC
    VECS = V_BP1 + 1

    beta_table = nc.dram_tensor("beta_table", (E, 2, D), f32, kind="Internal").ap()
    gate_table = nc.dram_tensor("gate_table", (B, D), f32, kind="Internal").ap()

    def tok(dram):
        return dram.rearrange("(t p) d -> p t d", p=P)

    with ExitStack() as ctx:
        def sb(name, shape, dt=f32):
            return ctx.enter_context(nc.sbuf_tensor(name, shape, dt))

        def bank(name):
            return ctx.enter_context(nc.psum_tensor(name, [P, 512], f32))

        def sem(name):
            return ctx.enter_context(nc.semaphore(name))

        ident = sb("ident", [P, P])
        ones_r = sb("ones_r", [P, P], f32r)
        vec_rows = sb("vec_rows", [VECS, P])
        vecs = sb("vecs", [P, VECS])
        keep = sb("keep", [P, DC])
        fresh = sb("fresh", [P, DC])
        mixT = sb("mixT", [P, DC, D])
        mix_w = sb("mix_w", [P, 2, DC, D], f32r)
        taps = sb("taps", [P, DC, TAPS])
        bias_bc = sb("bias_bc", [P, DC])
        wp1 = sb("wp1", [P, DC, NAV])
        wp2 = sb("wp2", [P, E])
        bp2_sb = sb("bp2_sb", [1, E])
        wo = sb("wo", [P, DC, D])
        bo_all = sb("bo_all", [E, D])
        c_nat = sb("c_nat", [B, D])
        sigmoid_cT = sb("sigmoid_cT", [P, DC, B])
        silu_cT = sb("silu_cT", [P, DC, B])
        mods = sb("mods", [P, B, MODS])
        gate_raw = sb("gate_raw", [P, DC, B])
        gate_sign = sb("gate_sign", [P, DC, B])
        gate_size = sb("gate_size", [P, DC, B])
        gate = sb("gate", [P, DC, B])
        gb_raw = sb("gb_raw", [B, D])
        gb_sign = sb("gb_sign", [B, D])
        gb_size = sb("gb_size", [B, D])
        gb_rows = sb("gb_rows", [B, D])
        beta = sb("beta", [E, D])
        beta3 = sb("beta3", [E, D])
        beta_parts = sb("beta_parts", [E, 2, D], f32r)
        up_all = sb("up_all", [P, E, UP])
        down_all = sb("down_all", [P, E, DOWN])
        eps_t = sb("eps_t", [P, TT])
        minus_half = sb("minus_half", [P, TT])
        minus_one = sb("minus_one", [P, TT])

        x_sb = sb("x_sb", [P, 2, TT, D])
        modc = sb("modc", [P, 2, MODS])
        st1 = sb("st1", [P, TT, 6])
        mv1 = sb("mv1", [P, TT, 2])
        ve1 = sb("ve1", [P, TT])
        rstd1 = sb("rstd1", [P, TT])
        mr1 = sb("mr1", [P, TT])
        nmr1 = sb("nmr1", [P, TT])
        xn1 = sb("xn1", [P, TT, D])
        h = sb("h", [P, DC, T + 2 * PAD])
        S = sb("S", [P, DC, T])
        S_hi = sb("S_hi", [P, DC, T], f32r)
        S_lo = sb("S_lo", [P, DC, T], f32r)
        r1T = sb("r1T", [P, DC, T])
        x1 = sb("x1", [P, 2, TT, D])
        st2 = sb("st2", [P, TT, 6])
        mv2 = sb("mv2", [P, TT, 2])
        ve2 = sb("ve2", [P, TT])
        rstd2 = sb("rstd2", [P, TT])
        mr2 = sb("mr2", [P, TT])
        nmr2 = sb("nmr2", [P, TT])
        xn2 = sb("xn2", [P, TT, D])
        hid = sb("hid", [P, 2, DC, T])
        hid_hi = sb("hid_hi", [P, DC, T], f32r)
        hid_lo = sb("hid_lo", [P, DC, T], f32r)
        nav = sb("nav", [P, 1])
        top8 = sb("top8", [1, 8])
        sel8 = sb("sel8", [1, 2, 8], u32)
        up_w = sb("up_w", [P, 2, UP], f32r)
        down_w = sb("down_w", [P, 2, DOWN], f32r)
        b1_w = sb("b1_w", [P, FC])
        beta_w = sb("beta_w", [P, 2, D], f32r)
        g = sb("g", [P, FC, T])
        g_hi = sb("g_hi", [P, FC, T], f32r)
        g_lo = sb("g_lo", [P, FC, T], f32r)
        gb_bc = sb("gb_bc", [P, 2, D])
        o_sb = sb("o_sb", [P, 2, TT, D])

        w_nat = S[:, :, 0:D]
        w2_nat = g[:, :, :].rearrange("p f t -> p (f t)").rearrange("p (q f d) -> p q f d", q=2, d=D)
        w2T = o_sb[:, :, :, :].rearrange("p q t d -> p (q t d)").rearrange("p (q c f) -> p q c f", q=2, f=F)
        wmod_room = x1[:, :, :, :].rearrange("p q t d -> p (q t d)")
        wmod_sb = [[wmod_room[:, 0:3 * D], wmod_room[:, 3 * D:6 * D]],
                   [xn2[:, :, :].rearrange("p t d -> p (t d)")[:, 0:3 * D], hid[:, 1].rearrange("p c t -> p (c t)")[:, 0:3 * D]]]

        Y = [bank("Y0"), bank("Y1")]
        TR = [bank("TR0"), bank("TR1")]
        U = [bank("U0"), bank("U1")]
        Q = [bank("Q0"), bank("Q1")]

        s_vecs = sem("s_vecs")
        s_c = sem("s_c")
        s_w = sem("s_w")
        s_wo = sem("s_wo")
        s_wmod = sem("s_wmod")
        s_small = sem("s_small")
        s_up = sem("s_up")
        s_w2 = [sem("s_w2a"), sem("s_w2b")]
        s_pool_const = sem("s_pool_const")
        s_pe_setup = sem("s_pe_setup")
        s_act_setup = sem("s_act_setup")
        s_dve_setup = sem("s_dve_setup")
        s_tables = sem("s_tables")
        s_mix_w = sem("s_mix_w")
        s_w2T_mm = sem("s_w2T_mm")
        s_w2T_cp = sem("s_w2T_cp")
        s_comb = sem("s_comb")
        s_down = sem("s_down")

        x_loaded = [sem("x_loaded0"), sem("x_loaded1")]
        gb_loaded = [sem("gb_loaded0"), sem("gb_loaded1")]
        beta_loaded = [sem("beta_loaded0"), sem("beta_loaded1")]
        up_hi_ready = sem("up_hi_ready")
        up_lo_ready = sem("up_lo_ready")
        b1_ready = sem("b1_ready")
        down_hi_ready = sem("down_hi_ready")
        down_lo_ready = sem("down_lo_ready")
        stored = [sem("stored0"), sem("stored1")]
        modc_ready = sem("modc_ready")
        dve_st1 = sem("dve_st1")
        stats1_ready = sem("stats1_ready")
        pool_rstd1 = sem("pool_rstd1")
        norm1_ready = sem("norm1_ready")
        xn1_ready = sem("xn1_ready")
        t1_done = sem("t1_done")
        h_ready = sem("h_ready")
        S_ready = sem("S_ready")
        S_hi_ready = sem("S_hi_ready")
        S_lo_ready = sem("S_lo_ready")
        mix_done = sem("mix_done")
        conv_step = [sem("conv_step0"), sem("conv_step1")]
        conv_done = sem("conv_done")
        r1_ready = sem("r1_ready")
        t2_done = sem("t2_done")
        x1_ready = sem("x1_ready")
        dve_st2 = sem("dve_st2")
        stats2_ready = sem("stats2_ready")
        pool_rstd2 = sem("pool_rstd2")
        norm2_ready = sem("norm2_ready")
        xn2_ready = sem("xn2_ready")
        t3_done = sem("t3_done")
        hid_ready = sem("hid_ready")
        r_nav = sem("r_nav")
        nav_ready = sem("nav_ready")
        r_logits = sem("r_logits")
        dve_router = sem("dve_router")
        sel_ready = sem("sel_ready")
        up_done = sem("up_done")
        gelu_out = sem("gelu_out")
        g_hi_ready = sem("g_hi_ready")
        g_lo_ready = sem("g_lo_ready")
        hid_hi_ready = sem("hid_hi_ready")
        hid_lo_ready = sem("hid_lo_ready")
        down_done = sem("down_done")
        scaled = sem("scaled")
        o_ready = [sem("o_ready0"), sem("o_ready1")]

        VECS_LOADED = 16 * 6
        SMALL_LOADED = 16 * 5
        GATES_DONE = 17 + DC
        SETUP_STEPS = GATES_DONE + 2 * DC + 4

        CONV_ORDER = sorted(((k, c) for k in range(TAPS) for c in range(DC)), key=lambda kc: DC * kc[0] + (DC + 1) * kc[1])

        EXPERTS_AT = {(-2, "middle"): (0,), (-1, "start"): (1, 2), (-1, "fill"): (3, 4), (-1, "middle"): (5,),
                      (0, "start"): (6,), (0, "fill"): (7,)}

        def experts_at(i, place):
            return EXPERTS_AT.get((i, place), ()) if isinstance(i, int) else ()

        def wait(eng, s, v):
            if not isinstance(v, int) or v > 0:
                eng.wait_ge(s, v)

        def snapped(eng, v):
            return v if isinstance(v, int) else eng.snap(eng.to_reg(v), min_val=0, max_val=4096)

        def slots(eng, slot):
            for i in range(-2, UNROLL):
                slot(i, i // 2, i % 2)
            with eng.Fori(1, B // UNROLL - 1) as m:
                for u in range(UNROLL):
                    slot(UNROLL * m + u, UNROLL // 2 * m + u // 2, u % 2)
            for i in range(B - UNROLL, B + 1):
                slot(i, i // 2, i % 2)

        def inside(i, off):
            return not isinstance(i, int) or 0 <= i + off < B

        block = ctx.enter_context(nc.Block())

        @block.sync
        def _(sp):
            def load_x(i, half, par):
                wait(sp, x1_ready, 2 * (i - 1))
                sp.dma_start(x_sb[:, par], tok(x[bass.ds(i, 1)].rearrange("o t d -> (o t) d"))).then_inc(x_loaded[par], 16)

            def rows(v, n):
                return vec_rows[v:v + n, :]

            for dst, src in [(rows(V_DECAY, DC), decay_logit.rearrange("(r p) -> r p", p=P)),
                             (rows(V_B, DC), b.rearrange("(r p) -> r p", p=P)),
                             (rows(V_CONV, DC), conv_b.rearrange("(r p) -> r p", p=P)),
                             (rows(V_B1, E * FC), b1.rearrange("e (r p) -> (e r) p", p=P)),
                             (rows(V_B2, E * DC), b2.rearrange("e (r p) -> (e r) p", p=P)),
                             (rows(V_BP1, 1), bp1.rearrange("(r p) -> r p", p=P))]:
                sp.dma_start(dst, src).then_inc(s_vecs, 16)
            load_x(0, 0, 0)
            sp.dma_start(wo[:, :, :], Wo.rearrange("(c p) d -> p c d", p=P)).then_inc(s_wo, 16)
            sp.dma_start(w_nat[:, :, :], W.rearrange("(c p) d -> p c d", p=P)).then_inc(s_w, 16)
            sp.dma_start(taps[:, :, :], conv_w.rearrange("(c p) o k -> p c (o k)", p=P)).then_inc(s_small, 16)
            sp.dma_start(wp1[:, :, :], Wp1.rearrange("(c p) n -> p c n", p=P)).then_inc(s_small, 16)
            sp.dma_start(wp2[:, :], Wp2).then_inc(s_small, 16)
            sp.dma_start(bp2_sb[:, :], bp2.rearrange("(o e) -> o e", o=1)).then_inc(s_small, 16)
            sp.dma_start(bo_all[:, :], bo.rearrange("(o d) -> o d", o=1).to_broadcast([E, D])).then_inc(s_small, 16)
            for e in range(E):
                if e == 2:
                    load_x(1, 0, 1)
                    sp.dma_start(up_all[:, :, :].rearrange("p e (c f) -> p (e c) f", c=DC),
                                 W1.rearrange("e d f -> (e d) f").rearrange("(g p) f -> p g f", p=P)).then_inc(s_up, 16)
                wait(sp, s_w2T_mm, e - 1)
                sp.dma_start(w2_nat[:, e % 2], W2[e].rearrange("(c p) d -> p c d", p=P)).then_inc(s_w2[e % 2], 16)
            sp.wait_ge(s_dve_setup, SETUP_STEPS)
            sp.dma_start(gate_table, gb_rows[:, :]).then_inc(s_tables, 16)
            sp.dma_start(beta_table, beta_parts[:, :, :].bitcast(f32)).then_inc(s_tables, 16)
            sp.wait_ge(s_tables, 32)
            load_x(2, 1, 0)

            def slot(i, half, par):
                if inside(i, 0):
                    used, chosen = snapped(sp, HB * (i - 1)), snapped(sp, i + 1)
                    sp.wait_ge(s_tables, 32)
                    wait(sp, down_done, used)
                    sp.wait_ge(sel_ready, chosen)
                    e = sp.value_load(sel8[0:1, par, 0:1], min_val=0, max_val=E - 1)
                    sp.dma_start(beta_w[0:2, par].bitcast(f32), beta_table[bass.ds(e, 1)].rearrange("o k d -> (o k) d")).then_inc(beta_loaded[par], 16)
                if inside(i, -1):
                    for k in range(HB):
                        sp.wait_ge(o_ready[k], i)
                        ts = slice(k * TPB, (k + 1) * TPB)
                        sp.dma_start(tok(out[bass.ds(i - 1, 1)].rearrange("o t d -> (o t) d"))[:, ts], o_sb[:, 1 - par, ts]).then_inc(stored[1 - par], 16)
                if inside(i, 1):
                    wait(sp, scaled, HB * i)
                    sp.dma_start(gb_bc[:, 1 - par], gate_table[bass.ds(i + 1, 1)].to_broadcast([P, D])).then_inc(gb_loaded[1 - par], 16)
                if inside(i, 3) and inside(i, 0):
                    load_x(i + 3, half + 1, 1 - par)

            slots(sp, slot)
            for q in stored:
                sp.wait_ge(q, 16 * HB * B // 2)

        @block.gpsimd
        def _(pool):
            nc.gpsimd.memset(ident[:, :], 0.0).then_inc(s_pool_const, 1)
            nc.gpsimd.memset(eps_t[:, :], EPS).then_inc(s_pool_const, 1)
            nc.gpsimd.memset(minus_half[:, :], -0.5).then_inc(s_pool_const, 1)
            nc.gpsimd.memset(minus_one[:, :], -1.0).then_inc(s_pool_const, 1)
            nc.gpsimd.memset(ones_r[:, :].bitcast(f32), 1.0).then_inc(s_pool_const, 1)
            nc.gpsimd.memset(beta_w[:, :, :].bitcast(f32), 0.0).then_inc(s_pool_const, 1)
            nc.gpsimd.memset(h[:, :, :], 0.0).then_inc(s_pool_const, 1)
            pool.wait_ge(s_pool_const, 7)
            nc.gpsimd.affine_select(out=ident[:, :], in_=ident[:, :], compare_op=ALU.not_equal, fill=1.0,
                                    base=0, pattern=[[-1, P]], channel_multiplier=1).then_inc(s_pool_const, 1)

            def norm_scale(b_, stats_ready, consumed, mv, ve, rstd, mr, nmr, steps, ready):
                pool.wait_ge(stats_ready, b_ + 1)
                wait(pool, consumed, TT * b_)
                nc.gpsimd.tensor_tensor(ve[:, :], mv[:, :, 1], eps_t[:, :], ALU.add).then_inc(steps, 1)
                pool.wait_ge(steps, 3 * b_ + 1)
                nc.gpsimd.tensor_tensor(rstd[:, :], ve[:, :], minus_half[:, :], ALU.pow).then_inc(steps, 1)
                pool.wait_ge(steps, 3 * b_ + 2)
                nc.gpsimd.tensor_tensor(mr[:, :], mv[:, :, 0], rstd[:, :], ALU.mult).then_inc(steps, 1)
                pool.wait_ge(steps, 3 * b_ + 3)
                nc.gpsimd.tensor_tensor(nmr[:, :], mr[:, :], minus_one[:, :], ALU.mult).then_inc(ready, 1)

            def slot(i, half, par):
                opp = 1 - par
                if inside(i, 0):
                    wait(pool, up_done, FC * i)
                    for c in range(DC):
                        pool.wait_ge(hid_hi_ready, DC * i + c + 1)
                        nc.gpsimd.tensor_tensor(hid_lo[:, c], hid[:, par, c], hid_hi[:, c].bitcast(f32),
                                                ALU.subtract).then_inc(hid_lo_ready, 1)

                if inside(i, 0):
                    chosen, up_hi, down_hi = snapped(pool, i + 1), snapped(pool, i + 1), snapped(pool, i + 1)
                    pool.wait_ge(s_up, 16)
                    pool.wait_ge(sel_ready, chosen)
                    e = pool.value_load(sel8[0:1, par, 0:1], min_val=0, max_val=E - 1)
                    pool.wait_ge(s_up, 16)
                    pool.wait_ge(up_hi_ready, up_hi)
                    nc.gpsimd.tensor_tensor(up_w[:, 1:2], up_all[:, bass.ds(e, 1)], up_w[:, 0:1].bitcast(f32),
                                            ALU.subtract).then_inc(up_lo_ready, 1)
                if inside(i, -1):
                    pool.wait_ge(scaled, HB * i)
                    ts = slice(TPB, TT)
                    nc.gpsimd.tensor_tensor(o_sb[:, opp, ts], o_sb[:, opp, ts], x1[:, opp, ts], ALU.add).then_inc(o_ready[1], 1)
                if inside(i, 0):
                    pool.wait_ge(s_down, 2 * E)
                    pool.wait_ge(down_hi_ready, down_hi)
                    nc.gpsimd.tensor_tensor(down_w[:, 1:2], down_all[:, bass.ds(e, 1)], down_w[:, 0:1].bitcast(f32),
                                            ALU.subtract).then_inc(down_lo_ready, 1)
                if inside(i, 1):
                    norm_scale(i + 1, stats2_ready, xn2_ready, mv2, ve2, rstd2, mr2, nmr2, pool_rstd2, norm2_ready)

                def g_low(first, last):
                    for f in range(first, last):
                        pool.wait_ge(g_hi_ready, FC * i + f + 1)
                        nc.gpsimd.tensor_tensor(g_lo[:, f], g[:, f], g_hi[:, f].bitcast(f32), ALU.subtract).then_inc(g_lo_ready, 1)

                if inside(i, 0):
                    wait(pool, down_done, HB * i)
                    g_low(0, GELU_HEAD)
                if inside(i, 3):
                    norm_scale(i + 3, stats1_ready, xn1_ready, mv1, ve1, rstd1, mr1, nmr1, pool_rstd1, norm1_ready)
                if inside(i, 0):
                    g_low(GELU_HEAD, FC)

            norm_scale(0, stats1_ready, xn1_ready, mv1, ve1, rstd1, mr1, nmr1, pool_rstd1, norm1_ready)
            slots(pool, slot)

        @block.scalar
        def _(act):
            act.dma_start(c_nat[:, :], c_in).then_inc(s_c, 16)
            for c in range(DC):
                for half in range(2):
                    act.dma_start(wmod_sb[c][half], wmod[c * P:(c + 1) * P, half * 3 * D:(half + 1) * 3 * D]).then_inc(s_wmod, 16)
            act.wait_ge(s_pe_setup, 1)
            for c in range(DC):
                nc.scalar.activation(sigmoid_cT[:, c], Y[0][:, c * B:(c + 1) * B], ACT.Sigmoid).then_inc(s_act_setup, 1)
            act.wait_ge(s_dve_setup, DC + 1)
            nc.scalar.activation(keep[:, :], vecs[:, V_DECAY:V_DECAY + DC], ACT.Sigmoid).then_inc(s_act_setup, 1)
            def normalise(b_, src, dst, rstd, nmr, scale_ready, used, ready):
                act.wait_ge(scale_ready, b_ + 1)
                wait(act, used, DC * b_)
                for j in range(TT):
                    nc.scalar.activation(dst[:, j], src[:, j], ACT.Identity, bias=nmr[:, j:j + 1],
                                         scale=rstd[:, j:j + 1]).then_inc(ready, 1)

            normalise(0, x_sb[:, 0], xn1, rstd1, nmr1, norm1_ready, t1_done, xn1_ready)
            act.wait_ge(s_dve_setup, DC + 2)
            act.wait_ge(s_pe_setup, 6)
            for c in range(DC):
                nc.scalar.activation(mixT[:, c], Y[1][:, c * D:(c + 1) * D], ACT.Copy,
                                     scale=fresh[:, c:c + 1]).then_inc(s_act_setup, 1)

            def expert(e):
                for k in range(2):
                    act.wait_ge(s_comb, 2 * e + k + 1)
                    nc.scalar.activation(down_all[:, e, k * DOWN // 2:(k + 1) * DOWN // 2], Q[k][:, :], ACT.Copy,
                                         scale=OUT_SCALE).then_inc(s_down, 1)

            def slot(i, half, par):
                opp = 1 - par
                for e in experts_at(i, "start"):
                    expert(e)
                if inside(i, 0):
                    act.wait_ge(r_nav, i + 1)
                    nc.scalar.activation(nav[:, :], TR[0][:, 0:1], ACT.Gelu, bias=vecs[:, V_BP1:V_BP1 + 1]).then_inc(nav_ready, 1)
                if inside(i, 2) and inside(i, 1):
                    normalise(i + 2, x_sb[:, par], xn1, rstd1, nmr1, norm1_ready, t1_done, xn1_ready)
                if inside(i, 0):
                    chosen = snapped(act, i + 1)
                    act.wait_ge(s_up, 16)
                    act.wait_ge(sel_ready, chosen)
                    expert_of_row = act.value_load(sel8[0:1, par, 0:1], min_val=0, max_val=E - 1)
                    up_used, low_used, bias_used, down_used = (snapped(act, FC * i), snapped(act, i), snapped(act, FC * i), snapped(act, HB * i))
                    act.wait_ge(s_up, 16)
                    wait(act, up_done, up_used)
                    wait(act, up_lo_ready, low_used)
                    nc.scalar.copy(up_w[:, 0:1], up_all[:, bass.ds(expert_of_row, 1)]).then_inc(up_hi_ready, 1)
                    act.wait_ge(s_up, 16)
                    wait(act, gelu_out, bias_used)
                    nc.scalar.copy(b1_w[:, :], b1_view[:, bass.ds(expert_of_row, 1)].rearrange("p o f -> p (o f)")).then_inc(b1_ready, 1)
                for e in experts_at(i, "fill"):
                    expert(e)
                if inside(i, 1):
                    wait(act, t2_done, HB * (i + 1))
                    for c in range(DC):
                        act.wait_ge(conv_done, DC * (i + 1) + c + 1)
                        nc.scalar.activation(r1T[:, c], Y[c][:, :], ACT.Identity, bias=modc[:, opp, GAB + c:GAB + c + 1],
                                             scale=modc[:, opp, GA + c:GA + c + 1]).then_inc(r1_ready, 1)
                if inside(i, 0):
                    act.wait_ge(s_down, 2 * E)
                    wait(act, down_done, down_used)
                    nc.scalar.copy(down_w[:, 0:1], down_all[:, bass.ds(expert_of_row, 1)]).then_inc(down_hi_ready, 1)
                if inside(i, 2):
                    wait(act, conv_done, DC * (i + 2))
                    act.wait_ge(modc_ready, i + 3)
                    for c in range(DC):
                        act.wait_ge(t1_done, DC * (i + 2) + c + 1)
                        nc.scalar.activation(h[:, c, PAD:PAD + T], Y[c][:, :], ACT.Identity, bias=modc[:, par, SA + c:SA + c + 1],
                                             scale=modc[:, par, CA + c:CA + c + 1]).then_inc(h_ready, 1)
                for e in experts_at(i, "middle"):
                    expert(e)

                def gelu(f):
                    act.wait_ge(up_done, FC * i + f + 1)
                    nc.scalar.activation(g[:, f], U[f % 2][:, :], ACT.Gelu,
                                         bias=b1_w[:, f:f + 1]).then_inc(gelu_out, 1)

                def high(f):
                    act.wait_ge(gelu_out, FC * i + f + 1)
                    nc.scalar.copy(g_hi[:, f], g[:, f]).then_inc(g_hi_ready, 1)

                if inside(i, 0):
                    act.wait_ge(b1_ready, i + 1)
                    wait(act, down_done, HB * i)
                    gelu(0)
                    high(0)
                    gelu(1)
                    high(1)
                    gelu(2)
                if inside(i, 1):
                    normalise(i + 1, x1[:, opp], xn2, rstd2, nmr2, norm2_ready, t3_done, xn2_ready)
                if inside(i, 0):
                    gelu(3)
                    high(2)
                    high(3)
                for e in experts_at(i, "end"):
                    expert(e)
                if inside(i, 1):
                    wait(act, down_done, HB * i)
                    for c in range(DC):
                        act.wait_ge(t3_done, DC * (i + 1) + c + 1)
                        nc.scalar.activation(hid[:, opp, c], TR[c][:, :], ACT.Identity, bias=modc[:, opp, SB + c:SB + c + 1],
                                             scale=modc[:, opp, CB + c:CB + c + 1]).then_inc(hid_ready, 1)
                    wait(act, hid_lo_ready, DC * (i + 1))
                    wait(act, up_done, FC * (i + 1))
                    for c in range(DC):
                        act.wait_ge(hid_ready, DC * (i + 1) + c + 1)
                        nc.scalar.copy(hid_hi[:, c], hid[:, opp, c]).then_inc(hid_hi_ready, 1)

            b1_view = vecs[:, V_B1:V_B1 + E * FC].rearrange("p (e f) -> p e f", f=FC)
            slots(act, slot)

        @block.vector
        def _(dve):
            step = [0]

            def done(ins):
                ins.then_inc(s_dve_setup, 1)
                step[0] += 1
                return step[0]

            for c in range(DC):
                dve.wait_ge(s_act_setup, DC)
                done(nc.vector.tensor_tensor(silu_cT[:, c], sigmoid_cT[:, c], Y[0][:, c * B:(c + 1) * B], ALU.mult))
            dve.wait_ge(s_pe_setup, 2)
            n = done(nc.vector.tensor_copy(vecs[:, :], U[1][:, 0:VECS]))
            dve.wait_ge(s_act_setup, DC + 1)
            done(nc.vector.tensor_scalar(fresh[:, :], keep[:, :], -1.0, 1.0, ALU.mult, ALU.add))
            dve.wait_ge(s_dve_setup, n)
            n = done(nc.vector.tensor_tensor(bias_bc[:, :], vecs[:, V_B:V_B + DC], vecs[:, V_CONV:V_CONV + DC], ALU.add))

            def mods_setup():
                dve.wait_ge(s_pe_setup, 3)
                view = TR[0][:, 0:5 * DC * B].rearrange("p (g c r) -> p g c r", g=5, c=DC)
                m4 = mods[:, :, :].rearrange("p r (g c) -> p g c r", c=DC)
                done(nc.vector.tensor_copy(m4[:, SA // DC], view[:, 0]))
                done(nc.vector.tensor_scalar_add(m4[:, CA // DC], view[:, 1], 1.0))
                done(nc.vector.tensor_copy(m4[:, SB // DC], view[:, 3]))
                done(nc.vector.tensor_scalar_add(m4[:, CB // DC], view[:, 4], 1.0))
                n = done(nc.vector.tensor_copy(gate_raw[:, :, :], view[:, 2]))
                dve.wait_ge(s_dve_setup, n)
                done(nc.vector.tensor_scalar(gate_sign[:, :, :], gate_raw[:, :, :], 0.0, 2.0, ALU.is_ge, ALU.mult))
                n = done(nc.vector.scalar_tensor_tensor(out=gate_size[:, :, :], in0=gate_raw[:, :, :], scalar=-1.0, in1=gate_raw[:, :, :], op0=ALU.mult, op1=ALU.max))
                dve.wait_ge(s_dve_setup, n)
                n = done(nc.vector.tensor_scalar_max(gate_size[:, :, :], gate_size[:, :, :], GATE_MIN))
                dve.wait_ge(s_dve_setup, n)
                n = done(nc.vector.scalar_tensor_tensor(out=gate[:, :, :], in0=gate_sign[:, :, :], scalar=-1.0,
                                                        in1=gate_size[:, :, :], op0=ALU.add, op1=ALU.mult))
                dve.wait_ge(s_dve_setup, n)
                for c in range(DC):
                    done(nc.vector.tensor_copy(mods[:, :, GA + c], gate[:, c, :]))
                    n = done(nc.vector.tensor_scalar(mods[:, :, GAB + c], gate[:, c, :], bias_bc[:, c:c + 1], None, ALU.mult))
                dve.wait_ge(s_dve_setup, n)

            def late_setup():
                dve.wait_ge(s_pe_setup, 4)
                n = done(nc.vector.tensor_copy(gb_raw[:, :], TR[1][0:B, 0:D]))
                dve.wait_ge(s_dve_setup, n)
                done(nc.vector.tensor_scalar(gb_sign[:, :], gb_raw[:, :], 0.0, 2.0, ALU.is_ge, ALU.mult))
                n = done(nc.vector.scalar_tensor_tensor(out=gb_size[:, :], in0=gb_raw[:, :], scalar=-1.0, in1=gb_raw[:, :], op0=ALU.mult, op1=ALU.max))
                dve.wait_ge(s_dve_setup, n)
                n = done(nc.vector.tensor_scalar_max(gb_size[:, :], gb_size[:, :], GATE_MIN))
                dve.wait_ge(s_dve_setup, n)
                n = done(nc.vector.scalar_tensor_tensor(out=gb_rows[:, :], in0=gb_sign[:, :], scalar=-1.0,
                                                        in1=gb_size[:, :], op0=ALU.add, op1=ALU.mult))
                dve.wait_ge(s_pe_setup, 5)
                dve.wait_ge(s_small, SMALL_LOADED)
                n = done(nc.vector.tensor_tensor(beta[:, :], TR[1][0:E, D:2 * D], bo_all[:, :], ALU.add))
                dve.wait_ge(s_dve_setup, n)
                n = done(nc.vector.tensor_scalar_mul(beta3[:, :], beta[:, :], OUT_SCALE))
                dve.wait_ge(s_dve_setup, n)
                n = done(nc.vector.tensor_copy(beta_parts[:, 0, :], beta3[:, :]))
                dve.wait_ge(s_dve_setup, n)
                n = done(nc.vector.tensor_tensor(beta_parts[:, 1, :], beta3[:, :], beta_parts[:, 0, :].bitcast(f32), ALU.subtract))
                dve.wait_ge(s_dve_setup, n)
                assert n == SETUP_STEPS


            def w2_copies(e):
                dve.wait_ge(s_w2T_mm, e + 1)
                wait(dve, s_comb, 2 * (e - 1))
                for c in range(DC):
                    nc.vector.tensor_copy(w2T[:, e % 2, c], U[c][:, :]).then_inc(s_w2T_cp, 1)

            def expert(e):
                if e + 1 < E:
                    w2_copies(e + 1)

            def conv(b_, first, last):
                for k, c in CONV_ORDER[first:last]:
                    if k == 0:
                        dve.wait_ge(mix_done, DC * b_ + c + 1)
                    else:
                        dve.wait_ge(conv_step[c], (TAPS - 1) * b_ + k)
                    ins = nc.vector.scalar_tensor_tensor(out=Y[c][:, :], in0=h[:, c, k:k + T], scalar=taps[:, c, k:k + 1],
                                                         in1=Y[c][:, :], op0=ALU.mult, op1=ALU.add)
                    ins.then_inc(conv_step[c] if k < TAPS - 1 else conv_done, 1)

            def router_max(b_):
                count = snapped(dve, b_ + 1)
                dve.wait_ge(s_pool_const, 8)
                dve.wait_ge(r_logits, count)
                nc.vector.max(top8[:, :], TR[0][0:1, 8:8 + E]).then_inc(dve_router, 1)

            def router_index(b_, par):
                count = snapped(dve, b_ + 1)
                dve.wait_ge(s_pool_const, 8)
                dve.wait_ge(dve_router, count)
                nc.vector.max_index(sel8[:, par], top8[:, :], TR[0][0:1, 8:8 + E]).then_inc(sel_ready, 1)

            def residual2(b_, half, par, k):
                ts = slice(k * TPB, (k + 1) * TPB)
                if k == 0:
                    dve.wait_ge(gb_loaded[par], 16 * (half + 1))
                    wait(dve, stored[par], 16 * HB * half)
                dve.wait_ge(down_done, HB * b_ + k + 1)
                nc.vector.tensor_tensor(o_sb[:, par, ts], Q[k][:, :].rearrange("p (t d) -> p t d", d=D),
                                        gb_bc[:, par:par + 1].to_broadcast([P, TPB, D]), ALU.mult).then_inc(scaled, 1)
                if k == 0:
                    dve.wait_ge(scaled, HB * b_ + 1)
                    nc.vector.tensor_tensor(o_sb[:, par, ts], o_sb[:, par, ts], x1[:, par, ts], ALU.add).then_inc(o_ready[0], 1)

            def modulation(b_, par):
                wait(dve, hid_ready, DC * (b_ - 1))
                nc.vector.tensor_copy(modc[:, par:par + 1, :], mods[:, bass.ds(b_, 1), :]).then_inc(modc_ready, 1)

            def stats1(b_, half, par):
                dve.wait_ge(x_loaded[par], 16 * (half + 1))
                for j in range(TT):
                    nc.vector.bn_stats(st1[:, j], x_sb[:, par, j]).then_inc(dve_st1, 1)
                used, full = snapped(dve, b_), snapped(dve, TT * (b_ + 1))
                dve.wait_ge(s_pool_const, 8)
                wait(dve, norm1_ready, used)
                dve.wait_ge(dve_st1, full)
                for j in range(TT):
                    ins = nc.vector.bn_aggr(mv1[:, j], st1[:, j])
                ins.then_inc(stats1_ready, 1)

            def residual1(b_, par):
                for k in range(HB):
                    ts = slice(k * TPB, (k + 1) * TPB)
                    wait(dve, o_ready[k], b_ - 1)
                    dve.wait_ge(t2_done, HB * b_ + k + 1)
                    nc.vector.tensor_tensor(x1[:, par, ts], x_sb[:, par, ts], TR[k][:, :].rearrange("p (t d) -> p t d", d=D),
                                            ALU.add).then_inc(x1_ready, 1)
                    dve.wait_ge(x1_ready, HB * b_ + k + 1)
                    for j in range(k * TPB, (k + 1) * TPB):
                        nc.vector.bn_stats(st2[:, j], x1[:, par, j]).then_inc(dve_st2, 1)
                used, full = snapped(dve, b_), snapped(dve, TT * (b_ + 1))
                dve.wait_ge(s_pool_const, 8)
                wait(dve, norm2_ready, used)
                dve.wait_ge(dve_st2, full)
                for j in range(TT):
                    ins = nc.vector.bn_aggr(mv2[:, j], st2[:, j])
                ins.then_inc(stats2_ready, 1)

            def scan(b_):
                wait(dve, S_lo_ready, DC * b_)
                for c in range(DC):
                    dve.wait_ge(h_ready, DC * b_ + c + 1)
                    nc.vector.tensor_tensor_scan(S[:, c], keep[:, c:c + 1].to_broadcast([P, T]), h[:, c, PAD:PAD + T],
                                                 0.0, ALU.mult, ALU.add).then_inc(S_ready, 1)
                wait(dve, mix_done, DC * b_)
                for c in range(DC):
                    dve.wait_ge(S_ready, DC * b_ + c + 1)
                    nc.vector.tensor_copy(S_hi[:, c], S[:, c]).then_inc(S_hi_ready, 1)
                for c in range(DC):
                    dve.wait_ge(S_hi_ready, DC * b_ + c + 1)
                    nc.vector.tensor_tensor(S_lo[:, c], S[:, c], S_hi[:, c].bitcast(f32), ALU.subtract).then_inc(S_lo_ready, 1)

            def slot(i, half, par):
                opp = 1 - par
                for e in experts_at(i, "start"):
                    expert(e)
                if inside(i, 1):
                    conv(i + 1, 0, CONV_HEAD)
                if inside(i, 0):
                    router_max(i)
                if inside(i, 1):
                    conv(i + 1, CONV_HEAD, CONV_HEAD + CONV_MID)
                if inside(i, 0):
                    router_index(i, par)
                for e in experts_at(i, "fill"):
                    expert(e)
                if inside(i, 1):
                    conv(i + 1, CONV_HEAD + CONV_MID, TAPS * DC)
                if inside(i, 2):
                    modulation(i + 2, par)
                if inside(i, -1):
                    for k in range(HB):
                        residual2(i - 1, half - 1 if par == 0 else half, opp, k)
                if inside(i, 1):
                    residual1(i + 1, opp)
                for e in experts_at(i, "middle"):
                    expert(e)
                if inside(i, 2):
                    scan(i + 2)
                if inside(i, 3):
                    stats1(i + 3, half + 2 if par else half + 1, opp)
                if isinstance(i, int) and i == -2:
                    late_setup()
                for e in experts_at(i, "end"):
                    expert(e)

            stats1(0, 0, 0)
            mods_setup()
            w2_copies(0)
            dve.wait_ge(s_act_setup, 1 + 2 * DC)
            nc.vector.tensor_copy(mix_w[:, 0], mixT[:, :, :]).then_inc(s_mix_w, 1)
            dve.wait_ge(s_mix_w, 1)
            nc.vector.tensor_tensor(mix_w[:, 1], mixT[:, :, :], mix_w[:, 0].bitcast(f32), ALU.subtract).then_inc(s_mix_w, 1)

            slots(dve, slot)

        @block.tensor
        def _(pe):
            mm = nc.tensor.matmul

            def w2_transposes(e):
                pe.wait_ge(s_w2[e % 2], 16 * (e // 2 + 1))
                pe.wait_ge(s_dve_setup, DC + 1)
                wait(pe, s_w2T_cp, DC * e)
                for c in range(DC):
                    for f in range(FC):
                        ins = nc.tensor.transpose(U[c][:, f * P:(f + 1) * P], w2_nat[:, e % 2, f, c * P:(c + 1) * P], ident[:, :])
                ins.then_inc(s_w2T_mm, 1)

            pe.wait_ge(s_pool_const, 8)
            pe.wait_ge(s_c, 16)
            for c in range(DC):
                ins = nc.tensor.transpose(Y[0][:, c * B:(c + 1) * B], c_nat[:, c * P:(c + 1) * P], ident[0:B, 0:B])
            ins.then_inc(s_pe_setup, 1)
            pe.wait_ge(s_vecs, VECS_LOADED)
            nc.tensor.transpose(U[1][:, 0:VECS], vec_rows[:, :], ident[0:VECS, 0:VECS]).then_inc(s_pe_setup, 1)
            pe.wait_ge(s_dve_setup, DC)
            pe.wait_ge(s_wmod, 16 * 2 * DC)
            for g in range(5):
                for d in range(DC):
                    col = (g * DC + d) * B
                    for c in range(DC):
                        ins = mm(TR[0][:, col:col + B], wmod_sb[c][g // 3][:, g % 3 * D + d * P:g % 3 * D + (d + 1) * P], silu_cT[:, c],
                                 start=(c == 0), stop=(c == DC - 1))
            ins.then_inc(s_pe_setup, 1)
            for c in range(DC):
                ins = mm(TR[1][0:B, 0:D], silu_cT[:, c], wmod_sb[c][1][:, 2 * D:3 * D], start=(c == 0), stop=(c == DC - 1))
            ins.then_inc(s_pe_setup, 1)
            b2_view = vecs[:, V_B2:V_B2 + E * DC].rearrange("p (e c) -> p e c", c=DC)
            pe.wait_ge(s_dve_setup, DC + 1)
            pe.wait_ge(s_wo, 16)
            for c in range(DC):
                ins = mm(TR[1][0:E, D:2 * D], b2_view[:, :, c], wo[:, c], start=(c == 0), stop=(c == DC - 1))
            ins.then_inc(s_pe_setup, 1)
            pe.wait_ge(s_w, 16)
            for d in range(DC):
                for e in range(DC):
                    ins = nc.tensor.transpose(Y[1][:, d * D + e * P:d * D + (e + 1) * P], w_nat[:, e, d * P:(d + 1) * P], ident[:, :])
            ins.then_inc(s_pe_setup, 1)
            w2_transposes(0)
            pe.wait_ge(s_act_setup, 1 + 2 * DC)

            def expert(e):
                if e + 1 < E:
                    w2_transposes(e + 1)
                pe.wait_ge(s_w2T_cp, DC * (e + 1))
                for k in range(2):
                    wait(pe, s_down, 2 * (e - 1) + k + 1 if e else 0)
                    for f in range(FC // 2):
                        fk = k * FC // 2 + f
                        for c in range(DC):
                            ins = mm(Q[k][:, f * D:(f + 1) * D], w2T[:, e % 2, c, fk * P:(fk + 1) * P], wo[:, c],
                                     start=(c == 0), stop=(c == DC - 1))
                    ins.then_inc(s_comb, 1)

            def three(out_, w_hi, w_lo, m_hi, m_lo, start, stop):
                mm(out_, w_lo, m_hi, start=start, stop=False)
                mm(out_, w_hi, m_lo, start=False, stop=False)
                return mm(out_, w_hi, m_hi, start=False, stop=stop)

            def down(b_, par, j, f0=0, f1=FC):
                k, t = j // TPB, j % TPB
                tj = slice(j * P, (j + 1) * P)
                cols = Q[k][:, t * D:(t + 1) * D]
                if f0 == 0:
                    mm(cols, ones_r[:, :], beta_w[:, par], start=True, stop=False)
                    for c in range(DC):
                        mm(Q[k][:, t * D + c * P:t * D + (c + 1) * P], hid[:, par, c, tj], ident[:, :], start=False, stop=False,
                           is_transpose=True)
                for f in range(f0, f1):
                    ins = three(cols, g_hi[:, f, tj], g_lo[:, f, tj], down_w[:, 0, f * D:(f + 1) * D],
                                down_w[:, 1, f * D:(f + 1) * D], False, f == FC - 1)
                if t == TPB - 1 and f1 == FC:
                    ins.then_inc(down_done, 1)

            def slot(i, half, par):
                opp = 1 - par
                for e in experts_at(i, "start"):
                    expert(e)
                if inside(i, -1):
                    pe.wait_ge(beta_loaded[opp], 16 * (half if par == 0 else half + 1))
                    pe.wait_ge(down_lo_ready, i)
                    pe.wait_ge(g_lo_ready, FC * (i - 1) + DOWN_HEAD)
                    wait(pe, scaled, HB * (i - 1))
                    down(i - 1, opp, 0, 0, DOWN_HEAD)
                if inside(i, 0):
                    pe.wait_ge(hid_ready, DC * (i + 1))
                    for c in range(DC):
                        ins = mm(TR[0][:, 0:1], wp1[:, c], hid[:, par, c, T - 1:T], start=(c == 0), stop=(c == DC - 1))
                    ins.then_inc(r_nav, 1)
                if inside(i, -1):
                    down(i - 1, opp, TPB, 0, DOWN_HEAD)
                if inside(i, 0):
                    pe.wait_ge(nav_ready, i + 1)
                    mm(TR[0][0:1, 8:8 + E], nav[:, :], wp2[:, :], start=True, stop=False)
                    mm(TR[0][0:1, 8:8 + E], ident[0:1, 0:1], bp2_sb[:, :], start=False, stop=True).then_inc(r_logits, 1)
                if inside(i, -1):
                    pe.wait_ge(g_lo_ready, FC * i - 1)
                    for j in range(0, TT, TPB):
                        down(i - 1, opp, j, DOWN_HEAD, FC - 1)
                    pe.wait_ge(g_lo_ready, FC * i)
                    for j in range(TT):
                        down(i - 1, opp, j, FC - 1 if j % TPB == 0 else 0, FC)
                for e in experts_at(i, "fill"):
                    expert(e)
                if isinstance(i, int) and i == -1:
                    pe.wait_ge(s_dve_setup, SETUP_STEPS)
                if inside(i, 1):
                    wait(pe, sel_ready, i + 1)
                    pe.wait_ge(r1_ready, DC * (i + 2))
                    for k in range(HB):
                        for t in range(TPB):
                            j = k * TPB + t
                            for c in range(DC):
                                ins = nc.tensor.transpose(TR[k][:, t * D + c * P:t * D + (c + 1) * P],
                                                          r1T[:, c, j * P:(j + 1) * P], ident[:, :])
                        ins.then_inc(t2_done, 1)
                if inside(i, 2):
                    wait(pe, r1_ready, DC * (i + 2))
                    for c in range(DC):
                        for j in range(TT):
                            if c == 0:
                                pe.wait_ge(xn1_ready, TT * (i + 2) + j + 1)
                            ins = nc.tensor.transpose(Y[c][:, j * P:(j + 1) * P], xn1[:, j, c * P:(c + 1) * P], ident[:, :])
                        ins.then_inc(t1_done, 1)
                for e in experts_at(i, "middle"):
                    expert(e)
                if inside(i, 0):
                    pe.wait_ge(up_lo_ready, i + 1)
                    pe.wait_ge(hid_lo_ready, DC * (i + 1))
                    for f in range(FC):
                        wait(pe, gelu_out, FC * i + f - 1)
                        for c in range(DC):
                            w = c * F + f * P
                            ins = three(U[f % 2][:, :], up_w[:, 0, w:w + P], up_w[:, 1, w:w + P],
                                        hid_hi[:, c], hid_lo[:, c], c == 0, c == DC - 1)
                        ins.then_inc(up_done, 1)
                for e in experts_at(i, "end"):
                    expert(e)

                def mix(e):
                    es = slice(e * P, (e + 1) * P)
                    for d in range(DC):
                        if e == 0:
                            pe.wait_ge(S_hi_ready, DC * (i + 2) + d + 1)
                        mm(Y[e][:, :], mix_w[:, 1, d, es], S_hi[:, d], start=(d == 0), stop=False)
                        mm(Y[e][:, :], mix_w[:, 0, d, es], S_hi[:, d], start=False, stop=False)
                    for d in range(DC):
                        if e == 0:
                            pe.wait_ge(S_lo_ready, DC * (i + 2) + d + 1)
                        ins = mm(Y[e][:, :], mix_w[:, 0, d, es], S_lo[:, d], start=False, stop=(d == DC - 1))
                    ins.then_inc(mix_done, 1)

                if isinstance(i, int) and i == -2:
                    pe.wait_ge(s_mix_w, 2)
                if inside(i, 2):
                    mix(0)
                if inside(i, 1):
                    for c in range(DC):
                        for j in range(TT):
                            if c == 0:
                                pe.wait_ge(xn2_ready, TT * (i + 1) + j + 1)
                            ins = nc.tensor.transpose(TR[c][:, j * P:(j + 1) * P], xn2[:, j, c * P:(c + 1) * P], ident[:, :])
                        ins.then_inc(t3_done, 1)
                if inside(i, 2):
                    mix(1)

            slots(pe, slot)


_INS = ['L0_attn_x', 'L0_attn_decay_logit', 'L0_attn_W', 'L0_attn_b', 'L0_attn_conv_w', 'L0_attn_conv_b',
        'L0_ffn_Wp1', 'L0_ffn_bp1', 'L0_ffn_Wp2', 'L0_ffn_bp2', 'L0_ffn_W1', 'L0_ffn_b1', 'L0_ffn_W2', 'L0_ffn_b2',
        'L0_ffn_Wo', 'L0_ffn_bo', 'L0_c', 'L0_wmod']
_OUTS = [((32, 512, 256), 'float32')]


def kernel(**inputs):
    import numpy as _np
    import concourse.bacc as _bacc
    from concourse import mybir as _mybir
    from concourse.bass_utils import run_bass_kernel_spmd as _run

    nc = _bacc.Bacc("TRN2", target_bir_lowering=False, num_devices=1)
    arrays, args = {}, []
    for name in _INS:
        a = _np.ascontiguousarray(inputs[name])
        arrays[f"in_{name}_dram"] = a
        args.append(nc.dram_tensor(f"in_{name}_dram", a.shape, _mybir.dt.from_np(a.dtype), kind="ExternalInput").ap())
    for i, (shape, dtype) in enumerate(_OUTS):
        dt = _mybir.dt.from_np(_np.dtype(dtype))
        args.append(nc.dram_tensor(f"out_{i}_dram", shape, dt, kind="ExternalOutput").ap())
    adaln_attention_ffn_kernel(nc, *args)
    r = _run(nc, [arrays], core_ids=[0])
    got = tuple(r.results[0][f"out_{i}_dram"] for i in range(len(_OUTS)))
    return got[0]
```
